# Optimizing a Trainium2 kernel written in Bass

```python
import numpy as np
import jax
import jax.numpy as jnp

def _softmax(x, axis=-1):
    return jax.nn.softmax(x, axis=axis)

def _gelu(x):
    return jax.nn.gelu(x, approximate=True)

def _silu(x):
    return jax.nn.silu(x)

def _sigmoid(x):
    return jax.nn.sigmoid(x)

def _layernorm(x, axis=-1, eps=1e-05):
    m = jnp.mean(x, axis=axis, keepdims=True)
    v = jnp.var(x, axis=axis, keepdims=True)
    return (x - m) / jnp.sqrt(v + eps)

def _scatter_add(tgt, idx, src, axis=0):
    return tgt.at[idx].add(src)

def _segment_sum(src, seg, n):
    return jax.ops.segment_sum(src, seg, n)
kernel_name = 'mk_seq_preln_d1_jaxref_r8_221f88'

def setup_inputs(seed: int=0):
    np.random.seed(seed)
    _w = jnp.asarray

    def _L0_attn_setup():
        import jax, jax.numpy as jnp
        import numpy as np
        EPS = 1e-05

        def layernorm(x, g, b):
            m = jnp.mean(x, axis=-1, keepdims=True)
            v = jnp.mean(jnp.square(x - m), axis=-1, keepdims=True)
            return (x - m) * jax.lax.rsqrt(v + EPS) * g + b

        def delta(x, gates_w, gates_b, lr_w, lr_b, out_w, out_b):
            N, T, C = x.shape
            qkv = x @ gates_w + gates_b
            q, k, v = jnp.split(qkv, 3, axis=-1)
            lr = x @ lr_w + lr_b
            k = k / jnp.linalg.norm(k, axis=-1, keepdims=True)
            K = jnp.tril(jnp.einsum('ntc,nsc->nts', k, k), k=-1)
            A = K + jnp.eye(T, dtype=x.dtype)
            u = jax.scipy.linalg.solve_triangular(A, v, lower=True)
            score = jnp.einsum('nsk,ntk->nst', q, k)
            y = jnp.einsum('nst,ntv->nsv', score, lr * u)
            return y @ out_w + out_b

        def mlp(x, w1, b1, w2, b2):
            return jax.nn.relu(x @ w1 + b1) @ w2 + b2
        N, T, C = (8, 256, 128)
        key = jax.random.key(seed)
        ks = jax.random.split(key, 16)
        s = 0.02
        return {'x': jax.random.normal(ks[0], (N, T, C), jnp.float32), 'dn_g': jnp.ones((C,), jnp.float32), 'dn_b': jnp.zeros((C,), jnp.float32), 'gates_w': jax.random.normal(ks[1], (C, 3 * C), jnp.float32) * s, 'gates_b': jnp.zeros((3 * C,), jnp.float32), 'lr_w': jax.random.normal(ks[2], (C, 1), jnp.float32) * s, 'lr_b': jnp.zeros((1,), jnp.float32), 'out_w': jax.random.normal(ks[3], (C, C), jnp.float32) * s, 'out_b': jnp.zeros((C,), jnp.float32), 'mn_g': jnp.ones((C,), jnp.float32), 'mn_b': jnp.zeros((C,), jnp.float32), 'w1': jax.random.normal(ks[4], (C, C), jnp.float32) * s, 'b1': jnp.zeros((C,), jnp.float32), 'w2': jax.random.normal(ks[5], (C, C), jnp.float32) * s, 'b2': jnp.zeros((C,), jnp.float32)}
    _L0_attn_in = _L0_attn_setup()

    def _L0_ffn_setup():
        import jax, jax.numpy as jnp
        import numpy as np
        B, S, H, E = (2, 1024, 128, 8)
        SCALE = 0.5
        key = jax.random.key(seed)
        k1, k2 = jax.random.split(key)
        x = jax.random.normal(k1, (B, S, H), dtype=jnp.float32)
        gate_w = jax.random.normal(k2, (E, H), dtype=jnp.float32) * 0.02
        coeff = SCALE * (1.0 + 0.05 * jnp.arange(E, dtype=jnp.float32))
        expert_w = coeff[:, None, None] * jnp.eye(H, dtype=jnp.float32)
        return {'x': x, 'gate_w': gate_w, 'expert_w': expert_w}
    _L0_ffn_in = _L0_ffn_setup()
    _d = {'L0_attn_x': _L0_attn_in['x'], 'L0_attn_dn_g': _L0_attn_in['dn_g'], 'L0_attn_dn_b': _L0_attn_in['dn_b'], 'L0_attn_gates_w': _L0_attn_in['gates_w'], 'L0_attn_gates_b': _L0_attn_in['gates_b'], 'L0_attn_lr_w': _L0_attn_in['lr_w'], 'L0_attn_lr_b': _L0_attn_in['lr_b'], 'L0_attn_out_w': _L0_attn_in['out_w'], 'L0_attn_out_b': _L0_attn_in['out_b'], 'L0_attn_mn_g': _L0_attn_in['mn_g'], 'L0_attn_mn_b': _L0_attn_in['mn_b'], 'L0_attn_w1': _L0_attn_in['w1'], 'L0_attn_b1': _L0_attn_in['b1'], 'L0_attn_w2': _L0_attn_in['w2'], 'L0_attn_b2': _L0_attn_in['b2'], 'L0_ffn_gate_w': _L0_ffn_in['gate_w'], 'L0_ffn_expert_w': _L0_ffn_in['expert_w']}
    _x0 = _d['L0_attn_x']
    _d['L0_attn_x'] = jax.random.normal(jax.random.fold_in(jax.random.key(seed), 1), (4, 1024, 128), dtype=_x0.dtype)
    del _x0
    return _d

def reference(L0_attn_x, L0_attn_dn_g, L0_attn_dn_b, L0_attn_gates_w, L0_attn_gates_b, L0_attn_lr_w, L0_attn_lr_b, L0_attn_out_w, L0_attn_out_b, L0_attn_mn_g, L0_attn_mn_b, L0_attn_w1, L0_attn_b1, L0_attn_w2, L0_attn_b2, L0_ffn_gate_w, L0_ffn_expert_w):

    def _L0_attn_ref(x, dn_g, dn_b, gates_w, gates_b, lr_w, lr_b, out_w, out_b, mn_g, mn_b, w1, b1, w2, b2):
        import jax, jax.numpy as jnp
        import numpy as np
        EPS = 1e-05

        def layernorm(x, g, b):
            m = jnp.mean(x, axis=-1, keepdims=True)
            v = jnp.mean(jnp.square(x - m), axis=-1, keepdims=True)
            return (x - m) * jax.lax.rsqrt(v + EPS) * g + b

        def delta(x, gates_w, gates_b, lr_w, lr_b, out_w, out_b):
            N, T, C = x.shape
            qkv = x @ gates_w + gates_b
            q, k, v = jnp.split(qkv, 3, axis=-1)
            lr = x @ lr_w + lr_b
            k = k / jnp.linalg.norm(k, axis=-1, keepdims=True)
            K = jnp.tril(jnp.einsum('ntc,nsc->nts', k, k), k=-1)
            A = K + jnp.eye(T, dtype=x.dtype)
            u = jax.scipy.linalg.solve_triangular(A, v, lower=True)
            score = jnp.einsum('nsk,ntk->nst', q, k)
            y = jnp.einsum('nst,ntv->nsv', score, lr * u)
            return y @ out_w + out_b

        def mlp(x, w1, b1, w2, b2):
            return jax.nn.relu(x @ w1 + b1) @ w2 + b2
        x = x + delta(layernorm(x, dn_g, dn_b), gates_w, gates_b, lr_w, lr_b, out_w, out_b)
        x = x + mlp(layernorm(x, mn_g, mn_b), w1, b1, w2, b2)
        return x

    def _L0_ffn_ref(x, gate_w, expert_w):
        import jax, jax.numpy as jnp
        import numpy as np
        B, S, H, E = (2, 1024, 128, 8)
        SCALE = 0.5
        scores = jnp.einsum('bsh,eh->bse', x, gate_w)
        chosen = jnp.argmax(scores, axis=-1)
        onehot = jax.nn.one_hot(chosen, gate_w.shape[0], dtype=x.dtype)
        expert_out = jnp.einsum('bsh,efh->bsef', x, expert_w)
        return x + jnp.einsum('bsef,bse->bsf', expert_out, onehot)
    x = L0_attn_x
    x = x + _L0_attn_ref(_layernorm(x, axis=-1), L0_attn_dn_g, L0_attn_dn_b, L0_attn_gates_w, L0_attn_gates_b, L0_attn_lr_w, L0_attn_lr_b, L0_attn_out_w, L0_attn_out_b, L0_attn_mn_g, L0_attn_mn_b, L0_attn_w1, L0_attn_b1, L0_attn_w2, L0_attn_b2)
    x = x + _L0_ffn_ref(_layernorm(x, axis=-1), L0_ffn_gate_w, L0_ffn_expert_w)
    return x

_drawn_inputs = setup_inputs


def setup_inputs(seed=0):
    import zlib

    import numpy as np

    out = dict(_drawn_inputs(seed))
    spreads = {'L0_attn_dn_g': (1.0, 0.6),
     'L0_attn_dn_b': (0.0, 0.8),
     'L0_attn_gates_b': (0.0, 0.1),
     'L0_attn_out_b': (0.0, 0.1),
     'L0_attn_mn_g': (1.0, 0.6),
     'L0_attn_mn_b': (0.0, 0.8),
     'L0_attn_b1': (0.0, 0.8),
     'L0_attn_b2': (0.0, 0.1)}
    factors = {'L0_attn_w1': 3.55, 'L0_attn_w2': 2.748, 'L0_ffn_gate_w': 3.439}
    for name, (base, spread) in spreads.items():
        noise = np.random.default_rng([zlib.crc32(name.encode()), seed]).standard_normal(out[name].shape)
        drawn = base * np.exp(spread * noise) if base else spread * noise
        out[name] = jnp.asarray(drawn.astype(out[name].dtype))
    for name, factor in factors.items():
        out[name] = (out[name] * factor).astype(out[name].dtype)
    return out
```

```python
from contextlib import ExitStack

import concourse.bass as bass
from concourse import mybir

P = 128
Q = 32
EPS = 1e-5

ALU = mybir.AluOpType
ACT = mybir.ActivationFunctionType
AX_X = mybir.AxisListType.X
F32 = mybir.dt.float32


def delta_block_kernel(
    nc: bass.Bass,
    x: bass.AP, dn_g: bass.AP, dn_b: bass.AP, gates_w: bass.AP, gates_b: bass.AP,
    lr_w: bass.AP, lr_b: bass.AP, out_w: bass.AP, out_b: bass.AP,
    mn_g: bass.AP, mn_b: bass.AP, w1: bass.AP, b1: bass.AP, w2: bass.AP, b2: bass.AP,
    gate_w: bass.AP, expert_w: bass.AP,
    out: bass.AP,
):
    NS, L, C = x.shape
    E, F, _ = expert_w.shape
    T = L // P
    NIT = T // 2
    NB = P // Q
    TN = T * NS
    KVW = 2 * C + 1
    EH = E // 2
    SET = 2 * NB
    assert C == P and F == P and NS == 4 and TN == Q and E == 8 and T % 2 == 0

    x_v = x.rearrange("n (t p) c -> p t n c", p=P)
    out_v = out.rearrange("n (t p) c -> p t n c", p=P)

    with ExitStack() as ctx:
        def sb(name, shape):
            return ctx.enter_context(nc.sbuf_tensor(name, shape, F32))

        def sem(name):
            return ctx.enter_context(nc.semaphore(name))

        def pair(name):
            return [sem(f"{name}{s}") for s in range(2)]

        def each(name):
            return [sem(f"{name}{n}") for n in range(NS)]

        ps = ctx.enter_context(nc.psum_tensor("ps", [P, 8, 512], F32))

        def tiles(bank, width=P):
            return ps[:, bank, 0:NS * width].rearrange("p (n c) -> p n c", n=NS)

        ident = sb("ident", [P, P])
        desc = sb("desc", [P, E])
        wq = sb("wq", [P, C])
        wqT = sb("wqT", [P, C])
        wkvl = sb("wkvl", [P, KVW])
        bkv = sb("bkv", [P, 2 * C])
        lrb = sb("lrb", [P, 1])
        wo = sb("wo", [P, C])
        bo = sb("bo", [P, C])
        w1s = sb("w1s", [P, C])
        w2s = sb("w2s", [P, C])
        b2s = sb("b2s", [P, C])
        cols = sb("cols", [P, 6])
        dng, dnb, mng, mnb, b1c, bqc = [cols[:, j:j + 1] for j in range(6)]
        bqB = sb("bqB", [P, P])
        gw = sb("gw", [E, C])
        gwT = sb("gwT", [P, E])
        ew = sb("ew", [P, E, C])
        ewT = sb("ewT", [P, E, F])

        x_all = sb("x_all", [P, T, NS, C])
        h_all = sb("h_all", [P, T, NS, C])
        xnT_all = sb("xnT_all", [P, T, NS * P])
        kv_all = sb("kv_all", [P, T, NS * 2 * C])
        g_all = sb("g_all", [P, T, NS * P])
        lr_all = sb("lr_all", [P, TN])
        gd_all = sb("gd_all", [P, Q, TN])
        lt = sb("lt", [P, Q, Q])
        xi = sb("xi", [P, Q, Q])
        prod = sb("prod", [P, Q * Q])
        dT_all = sb("dT_all", [P, Q, TN])
        d_all = sb("d_all", [P, Q, TN])

        st = [sb(f"st{s}", [P, NS, 6]) for s in range(2)]
        mv = [sb(f"mv{s}", [P, NS, 2]) for s in range(2)]
        ab = [sb(f"ab{s}", [P, 2, NS]) for s in range(2)]
        sd = [sb(f"sd{s}", [P, 2, NS]) for s in range(2)]
        rr = [sb(f"rr{s}", [P, 2, NS]) for s in range(2)]
        nb = [sb(f"nb{s}", [P, NS]) for s in range(2)]
        xh = [sb(f"xh{s}", [P, NS, C]) for s in range(2)]
        xnT = [sb(f"xnT{s}", [P, NS * P]) for s in range(2)]
        kv = [sb(f"kv{s}", [P, NS, 2 * C]) for s in range(2)]
        sq = sb("sq", [P, NS, C])
        ss = [sb(f"ss{s}", [P, NS]) for s in range(2)]
        sn = [sb(f"sn{s}", [P, NS]) for s in range(2)]
        rn = [sb(f"rn{s}", [P, NS]) for s in range(2)]
        kT = [sb(f"kT{s}", [P, NS * P]) for s in range(2)]
        gg = [sb(f"gg{s}", [P, NS, P]) for s in range(2)]

        kvs = [sb(f"kvs{s}", [P, NS, 2 * C]) for s in range(2)]
        gs = [sb(f"gs{s}", [P, NS, P]) for s in range(2)]
        lrs = [sb(f"lrs{s}", [P, NS]) for s in range(2)]
        tt = [sb(f"tt{s}", [P, NS, P]) for s in range(2)]
        da = [sb(f"da{s}", [P, NS, 2 * Q]) for s in range(2)]
        yT = [sb(f"yT{s}", [P, NS, Q]) for s in range(2)]
        y64 = [sb(f"y64{s}", [2 * Q, NS, 2 * Q]) for s in range(2)]
        wT = [sb(f"wT{s}", [P, NS, P]) for s in range(2)]
        uu = sb("uu", [P, NS, 2 * C])
        sm = sb("sm", [P, NS, 2 * C])

        mT = sb("mT", [P, NS * C])
        mw = sb("mw", [P, NS * C])
        gn = sb("gn", [P, NS, C])
        cb = sb("cb", [P, NS, C])

        xns = [sb(f"xns{s}", [P, NS, P]) for s in range(2)]
        hcb, tn, z = xh, xnT, kT
        tnv = [t[:, :].rearrange("p (n c) -> p n c", n=NS) for t in tn]
        zv = [t[:, :].rearrange("p (n c) -> p n c", n=NS) for t in z]
        tT = gg
        h2 = [kv[s][:, 0:2, :].rearrange("p a (b c) -> p (a b) c", b=2) for s in range(2)]
        x1 = [kv[s][:, 2:4, :].rearrange("p a (b c) -> p (a b) c", b=2) for s in range(2)]
        xb = gs
        hid = wT
        zT = tt
        xz = [kvs[s][:, 0:2, :].rearrange("p a (b c) -> p (a b) c", b=2) for s in range(2)]
        os_ = [kvs[s][:, 2:4, :].rearrange("p a (b c) -> p (a b) c", b=2) for s in range(2)]
        mx = [sb(f"mx{s}", [P, NS]) for s in range(2)]
        eq = [sb(f"eq{s}", [P, NS, E]) for s in range(2)]
        m2 = [sb(f"m2{s}", [P, NS]) for s in range(2)]
        oh = [sb(f"oh{s}", [P, NS, E]) for s in range(2)]
        ea, ed = [[t[:, :, :].rearrange("p a b -> p (a b)")[:, b * EH * F:(b + 1) * EH * F].rearrange("p (e f) -> p e f", e=EH)
                   for b in range(2)] for t in (gd_all, lt)]

        x_loaded, x_rest, w_loaded, e_loaded = pair("x_loaded"), sem("x_rest"), sem("w_loaded"), sem("e_loaded")
        id_zero, id_ready, consts_ready = sem("id_zero"), sem("id_ready"), sem("consts_ready")
        bqB_ready, wqT_mm, wqT_ready = sem("bqB_ready"), sem("wqT_mm"), sem("wqT_ready")
        stats_done, mv_done, var_done, ab_done = sem("stats_done"), sem("mv_done"), sem("var_done"), sem("ab_done")
        sd_done, rr_done, nb_done, h_done = sem("sd_done"), sem("rr_done"), sem("nb_done"), pair("h_done")
        xh_ready, xT_mm, xnT_ready, xnT_kept = sem("xh_ready"), pair("xT_mm"), sem("xnT_ready"), pair("xnT_kept")
        kv_mm, kv_ready, lr_ready = pair("kv_mm"), pair("kv_ready"), sem("lr_ready")
        ss_done, sn_done, rn_done, k_ready, kv_kept = (sem("ss_done"), sem("sn_done"), pair("rn_done"),
                                                       sem("k_ready"), pair("kv_kept"))
        kT_mm, kT_ready, g_mm, g_ready, g_kept, gd_done = (pair("kT_mm"), sem("kT_ready"), pair("g_mm"),
                                                           sem("g_ready"), pair("g_kept"), pair("gd_done"))
        xi_ready, lt_done, elim, dT_done, d_done = (sem("xi_ready"), sem("lt_done"), sem("elim"), sem("dT_done"),
                                                    sem("d_done"))
        ewT_mm, ewT_ready, gwT_ready = sem("ewT_mm"), sem("ewT_ready"), sem("gwT_ready")
        kvs_loaded, gs_loaded, blocks_set = pair("kvs_loaded"), pair("gs_loaded"), sem("blocks_set")
        ya_mm, yb_mm, ya_ready, yb_ready = sem("ya_mm"), sem("yb_mm"), sem("ya_ready"), sem("yb_ready")
        za_mm, zb_mm, za_ready, zb_ready = pair("za_mm"), pair("zb_mm"), sem("za_ready"), sem("zb_ready")
        y64_mm, y64_ready, t12_mm, t12_ready = pair("y64_mm"), sem("y64_ready"), pair("t12_mm"), sem("t12_ready")
        wT_mm, wT_ready = pair("wT_mm"), sem("wT_ready")
        u_mm, u_ready, lru_ready, sm_ready = each("u_mm"), each("u_ready"), each("lru_ready"), each("sm_ready")
        sm_mm = [pair(f"sm_mm{n}_") for n in range(NS)]
        fold_mm, fold_out, cb_ready = sem("fold_mm"), sem("fold_out"), sem("cb_ready")
        xns_loaded, dl_mm, hcb_ready, h2_ready = pair("xns_loaded"), pair("dl_mm"), sem("hcb_ready"), pair("h2_ready")
        tn_ready, tT_mm, tT_ready, xb_set, xb_ready = (sem("tn_ready"), pair("tT_mm"), sem("tT_ready"),
                                                       sem("xb_set"), pair("xb_ready"))
        hid_mm, hid_ready, out_mm, x1_ready = pair("hid_mm"), sem("hid_ready"), pair("out_mm"), pair("x1_ready")
        z_ready, zT_mm, zT_ready, xz_ready = sem("z_ready"), pair("zT_mm"), sem("zT_ready"), pair("xz_ready")
        gate_mm, oh_step, oh_ready = sem("gate_mm"), pair("oh_step"), sem("oh_ready")
        ea_mm, ed_mm, ea_done, ed_done = pair("ea_mm"), pair("ed_mm"), pair("ea_done"), pair("ed_done")
        add_step, stored = pair("add_step"), pair("stored")

        dve_passed, pe_passed = sem("dve_passed"), sem("pe_passed")

        block = ctx.enter_context(nc.Block())

        def earlier(eng, semaphore, value):
            if not isinstance(value, int) or value > 0:
                eng.wait_ge(semaphore, value)

        def norms(i, s, second):
            return T + 2 * (2 * i + s) + second

        def after(i, s):
            return (i, 1) if s == 0 else (i + 1, 0)

        def two_ahead(eng, first, body):
            first()
            body(0, 0, True, True)
            body(0, 1, True, True)
            with eng.Fori(1, NIT - 1) as i:
                body(i, 0, True, True)
                body(i, 1, True, True)
            body(NIT - 1, 0, False, True)
            body(NIT - 1, 1, False, False)

        def in_turn(eng, body):
            body(0, 0)
            body(0, 1)
            with eng.Fori(1, NIT) as i:
                body(i, 0)
                body(i, 1)

        @block.sync
        def _(sp):
            sp.dma_start(x_all[:, 0], x_v[:, 0]).then_inc(x_loaded[0], 16)
            for dst, src in ((wkvl[:, 0:2 * C], gates_w[:, C:3 * C]), (wkvl[:, 2 * C:KVW], lr_w),
                             (wq[:, :], gates_w[:, 0:C]), (wo[:, :], out_w), (w1s[:, :], w1), (w2s[:, :], w2),
                             (bkv[:, :], gates_b[C:3 * C].partition_broadcast(P)),
                             (lrb[:, :], lr_b.partition_broadcast(P)),
                             (bo[:, :], out_b.partition_broadcast(P)), (b2s[:, :], b2.partition_broadcast(P)),
                             (dng, dn_g.unsqueeze(1)), (dnb, dn_b.unsqueeze(1)), (mng, mn_g.unsqueeze(1)),
                             (mnb, mn_b.unsqueeze(1)), (b1c, b1.unsqueeze(1)), (bqc, gates_b[0:C].unsqueeze(1))):
                sp.dma_start(dst, src).then_inc(w_loaded, 16)
            for t in range(1, T):
                sp.dma_start(x_all[:, t], x_v[:, t]).then_inc(x_loaded[1] if t == 1 else x_rest, 16)
            sp.dma_start(gw[:, :], gate_w).then_inc(e_loaded, 16)
            sp.dma_start(ew[:, :, :], expert_w.rearrange("e f h -> f e h")).then_inc(e_loaded, 16)

            def keep_xn(i, s):
                sp.wait_ge(x_loaded[0], 16)
                sp.wait_ge(xnT_ready, 2 * i + s + 1)
                sp.dma_start(xnT_all[:, 2 * i + s, :], xnT[s][:, :]).then_inc(xnT_kept[s], 16)

            def body1(i, s, ahead2, ahead1):
                if ahead1:
                    keep_xn(*after(i, s))
                sp.wait_ge(x_loaded[0], 16)
                sp.wait_ge(k_ready, 2 * i + s + 1)
                sp.dma_start(kv_all[:, 2 * i + s, :], kv[s][:, :, :].rearrange("p n c -> p (n c)")).then_inc(kv_kept[s], 16)
                sp.wait_ge(x_loaded[0], 16)
                sp.wait_ge(g_ready, 2 * i + s + 1)
                sp.dma_start(g_all[:, 2 * i + s, :], gg[s][:, :, :].rearrange("p n c -> p (n c)")).then_inc(g_kept[s], 16)

            two_ahead(sp, lambda: keep_xn(0, 0), body1)
            for s in range(2):
                sp.wait_ge(kv_kept[s], 16 * NIT)
                sp.wait_ge(g_kept[s], 16 * NIT)
                sp.wait_ge(xnT_kept[s], 16 * NIT)

            def stage2(i, s):
                sp.wait_ge(x_loaded[0], 16)
                earlier(sp, sm_mm[NS - 1][s], i)
                earlier(sp, y64_mm[s], i)
                sp.dma_start(gs[s][:, :, :].rearrange("p n c -> p (n c)"), g_all[:, 2 * i + s, :]).then_inc(gs_loaded[s], 16)
                sp.dma_start(kvs[s][:, :, :].rearrange("p n c -> p (n c)"), kv_all[:, 2 * i + s, :]).then_inc(kvs_loaded[s], 16)

            in_turn(sp, stage2)

            def stage3(i, s):
                sp.wait_ge(x_loaded[0], 16)
                earlier(sp, dl_mm[s], i)
                sp.dma_start(xns[s][:, :, :].rearrange("p n c -> p (n c)"), xnT_all[:, 2 * i + s, :]).then_inc(xns_loaded[s], 16)

            def store(i, s):
                sp.wait_ge(x_loaded[0], 16)
                for b in range(2):
                    sp.wait_ge(add_step[b], 4 * (4 * i + 2 * s + 2))
                sp.dma_start(out_v[:, 2 * i + s], os_[s]).then_inc(stored[s], 16)

            def body3(i, s, ahead2, ahead1):
                if ahead1:
                    stage3(*after(i, s))
                store(i, s)

            two_ahead(sp, lambda: stage3(0, 0), body3)
            for s in range(2):
                sp.wait_ge(stored[s], 16 * NIT)

        @block.gpsimd
        def _(pool):
            nc.gpsimd.memset(ident[:], 0.0).then_inc(id_zero, 1)
            nc.gpsimd.memset(xi[:], 0.0).then_inc(id_zero, 1)
            pool.wait_ge(id_zero, 2)
            nc.gpsimd.affine_select(out=ident[:], in_=ident[:], compare_op=ALU.not_equal, fill=1.0, base=0,
                                    pattern=[[-1, P]], channel_multiplier=1).then_inc(id_ready, 1)
            nc.gpsimd.affine_select(out=xi[:], in_=xi[:], compare_op=ALU.not_equal, fill=1.0, base=0,
                                    pattern=[[1, Q], [-1, Q]], channel_multiplier=0).then_inc(xi_ready, 1)
            for e in range(E):
                nc.gpsimd.memset(desc[:, e:e + 1], float(E - e)).then_inc(consts_ready, 1)
            for s in range(2):
                nc.gpsimd.memset(tt[s][:], 0.0).then_inc(consts_ready, 1)
                nc.gpsimd.memset(da[s][:], 0.0).then_inc(consts_ready, 1)

            pool.wait_ge(xi_ready, 1)
            pool.wait_ge(consts_ready, E + 4)

            def diagonals(i, s):
                pool.wait_ge(g_ready, 2 * i + s + 1)
                for b in range(NB):
                    r = slice(Q * b, Q * b + Q)
                    nc.gpsimd.tensor_copy(
                        gd_all[r, :, bass.ds((2 * i + s) * NS, NS)].rearrange("p c n -> p n c"),
                        gg[s][r, :, Q * b:Q * b + Q]).then_inc(gd_done[s], 1)
                    pool.wait_ge(gd_done[s], NB * i + b + 1)

            in_turn(pool, diagonals)

            pool.wait_ge(dT_done, 1)
            pool.wait_ge(d_done, 1)

            def blocks(i, s):
                earlier(pool, wT_mm[s], i)
                earlier(pool, t12_mm[s], i)
                earlier(pool, sm_mm[NS - 1][s], i)
                at = bass.ds((2 * i + s) * NS, NS)
                for b in range(NB):
                    r = slice(Q * b, Q * b + Q)
                    nc.gpsimd.tensor_copy(tt[s][r, :, Q * b:Q * b + Q],
                                          dT_all[r, :, at].rearrange("p r n -> p n r")).then_inc(blocks_set, 1)
                    pool.wait_ge(blocks_set, SET * (2 * i + s) + 2 * b + 1)
                    if b < 3:
                        nc.gpsimd.tensor_copy(da[s][r, :, Q * (b % 2):Q * (b % 2) + Q],
                                              d_all[r, :, at].rearrange("p r n -> p n r")).then_inc(blocks_set, 1)
                        pool.wait_ge(blocks_set, SET * (2 * i + s) + 2 * b + 2)
                nc.gpsimd.tensor_copy(lrs[s][:, :], lr_all[:, at]).then_inc(blocks_set, 1)
                pool.wait_ge(blocks_set, SET * (2 * i + s + 1))

            in_turn(pool, blocks)

            b2B = b2s[:, :].unsqueeze(1).broadcast_to([P, NS, C])
            pool.wait_ge(cb_ready, 1)

            def front_a(i, s):
                earlier(pool, h2_ready[s], i)
                nc.gpsimd.tensor_tensor(hcb[s][:], h_all[:, 2 * i + s], cb[:], ALU.add).then_inc(hcb_ready, 1)
                earlier(pool, x1_ready[s], i)
                nc.gpsimd.tensor_tensor(xb[s][:], x_all[:, 2 * i + s], b2B, ALU.add).then_inc(xb_set, 1)

            def front_b(i, s):
                pool.wait_ge(xb_set, 2 * i + s + 1)
                pool.wait_ge(h2_ready[s], i + 1)
                nc.gpsimd.tensor_tensor(xb[s][:], xb[s][:], h2[s], ALU.add).then_inc(xb_ready[s], 1)

            def front_c(i, s):
                pool.wait_ge(z_ready, 2 * i + s + 1)
                nc.gpsimd.tensor_tensor(xz[s], x1[s], zv[s], ALU.add).then_inc(xz_ready[s], 1)

            def total(i, s, n):
                b, k = n % 2, 4 * i + 2 * s + n // 2
                pool.wait_ge(ea_done[b], k + 1)
                pool.wait_ge(ed_done[b], k + 1)
                nc.gpsimd.tensor_tensor(ea[b], ea[b], ed[b], ALU.add).then_inc(add_step[b], 1)
                pool.wait_ge(add_step[b], 4 * k + 1)
                nc.gpsimd.tensor_tensor(ea[b][:, 0:2], ea[b][:, 0:2], ea[b][:, 2:4], ALU.add).then_inc(add_step[b], 1)
                pool.wait_ge(add_step[b], 4 * k + 2)
                nc.gpsimd.tensor_tensor(ea[b][:, 0], ea[b][:, 0], ea[b][:, 1], ALU.add).then_inc(add_step[b], 1)
                pool.wait_ge(add_step[b], 4 * k + 3)
                if n == 0:
                    pool.wait_ge(xz_ready[s], i + 1)
                    earlier(pool, stored[s], 16 * i)
                nc.gpsimd.tensor_tensor(os_[s][:, n], ea[b][:, 0], xz[s][:, n], ALU.add).then_inc(add_step[b], 1)

            def body3(i, s, ahead2, ahead1):
                if ahead1:
                    front_a(*after(i, s))
                total(i, s, 0)
                if ahead1:
                    front_b(*after(i, s))
                total(i, s, 1)
                total(i, s, 2)
                total(i, s, 3)
                if ahead1:
                    front_c(*after(i, s))

            def first3():
                front_a(0, 0)
                front_b(0, 0)
                front_c(0, 0)

            two_ahead(pool, first3, body3)

        @block.scalar
        def _(act):
            act.wait_ge(w_loaded, 16 * 16)

            def roots1(i, s):
                act.wait_ge(ab_done, 2 * i + s + 1)
                nc.scalar.activation(sd[s][:], ab[s][:], ACT.Sqrt).then_inc(sd_done, 1)

            def h1(i, s):
                act.wait_ge(nb_done, 2 * i + s + 1)
                for n in range(NS):
                    last = nc.scalar.activation(h_all[:, 2 * i + s, n], x_all[:, 2 * i + s, n], ACT.Identity,
                                                bias=nb[s][:, n:n + 1], scale=rr[s][:, 0, n:n + 1])
                last.then_inc(h_done[s], 1)

            def xn1(i, s):
                act.wait_ge(xT_mm[s], i + 1)
                earlier(act, kv_mm[s], NS * i)
                earlier(act, xnT_kept[s], 16 * i)
                nc.scalar.activation(xnT[s][:], ps[:, 0, :], ACT.Identity, bias=dnb, scale=dng).then_inc(xnT_ready, 1)

            def norms1(i, s):
                earlier(act, rn_done[s], i)
                for n in range(NS):
                    act.wait_ge(kv_ready[s], NS * i + n + 1)
                    last = nc.scalar.activation(sq[:, n], kv[s][:, n, 0:C], ACT.Square, accum_out=ss[s][:, n:n + 1])
                last.then_inc(ss_done, 1)
                act.wait_ge(ss_done, 2 * i + s + 1)
                nc.scalar.activation(sn[s][:], ss[s][:], ACT.Sqrt).then_inc(sn_done, 1)

            def kT1(i, s):
                act.wait_ge(kT_mm[s], i + 1)
                earlier(act, g_mm[s], i)
                nc.scalar.copy(kT[s][:], ps[:, 5, :]).then_inc(kT_ready, 1)

            def first1():
                roots1(0, 0)
                h1(0, 0)
                roots1(0, 1)
                h1(0, 1)
                xn1(0, 0)
                norms1(0, 0)

            def body1(i, s, ahead2, ahead1):
                if ahead2:
                    roots1(i + 1, s)
                kT1(i, s)
                if ahead1:
                    xn1(*after(i, s))
                if ahead2:
                    h1(i + 1, s)
                if ahead1:
                    norms1(*after(i, s))

            two_ahead(act, first1, body1)

            act.wait_ge(wqT_mm, 1)
            nc.scalar.copy(wqT[:], ps[:, 0, 0:C])
            nc.scalar.copy(gwT[:], ps[:, 0, C:C + E]).then_inc(wqT_ready, 1)
            act.wait_ge(ewT_mm, 2)
            for q in range(2):
                last = nc.scalar.copy(ewT[:, EH * q:EH * q + EH, :].rearrange("p e f -> p (e f)"), ps[:, 1 + q, :])
            last.then_inc(ewT_ready, 1)

            def ya(i, s):
                act.wait_ge(ya_mm, 2 * i + s + 1)
                earlier(act, za_mm[s], i)
                nc.scalar.copy(yT[s][0:Q], ps[0:Q, 0, 0:NS * Q]).then_inc(ya_ready, 1)

            def za(i, s):
                act.wait_ge(za_mm[s], i + 1)
                nc.scalar.mul(tt[s][0:Q, :, Q:2 * Q], ps[0:Q, 0, NS * Q:2 * NS * Q].rearrange("p (n c) -> p n c", n=NS), -1.0)
                nc.scalar.mul(da[s][Q:2 * Q, :, 0:Q], ps[Q:2 * Q, 0, 2 * NS * Q:3 * NS * Q].rearrange("p (n c) -> p n c", n=NS),
                              -1.0).then_inc(za_ready, 1)

            def y64_(i, s):
                act.wait_ge(y64_mm[s], i + 1)
                earlier(act, t12_mm[s], i)
                nc.scalar.copy(y64[s][:], ps[0:2 * Q, 2, 0:2 * NS * Q]).then_inc(y64_ready, 1)

            def wT_(i, s):
                act.wait_ge(wT_mm[s], i + 1)
                earlier(act, u_mm[NS - 1], 2 * i)
                nc.scalar.mul(wT[s][:], ps[:, 5, :], -1.0).then_inc(wT_ready, 1)

            def u_(i, s, n):
                act.wait_ge(u_mm[n], 2 * i + s + 1)
                earlier(act, sm_mm[n][1 - s], i + s)
                nc.scalar.copy(uu[:, n, 0:C], tiles(3 + n % 2)[:, n]).then_inc(u_ready[n], 1)

            def first2():
                ya(0, 0)
                za(0, 0)
                y64_(0, 0)
                wT_(0, 0)

            def body2(i, s, ahead2, ahead1):
                u_(i, s, 0)
                u_(i, s, 1)
                if ahead1:
                    ya(*after(i, s))
                u_(i, s, 2)
                u_(i, s, 3)
                if ahead1:
                    za(*after(i, s))
                    y64_(*after(i, s))
                    wT_(*after(i, s))

            two_ahead(act, first2, body2)

            act.wait_ge(fold_mm, 1)
            nc.scalar.copy(mT[:], ps[:, 0, :]).then_inc(fold_out, 1)
            act.wait_ge(fold_mm, 2)
            nc.scalar.copy(mw[:], ps[:, 1, :]).then_inc(fold_out, 1)
            act.wait_ge(fold_mm, 3)
            nc.scalar.copy(gn[:].rearrange("p n c -> p (n c)"), ps[:, 2, :]).then_inc(fold_out, 1)

            def root(i, s, second):
                act.wait_ge(var_done, norms(i, s, second) + 1)
                nc.scalar.activation(sd[s][:, 0], ab[s][:, 0], ACT.Sqrt).then_inc(sd_done, 1)

            def tT_(i, s):
                act.wait_ge(tT_mm[s], i + 1)
                earlier(act, hid_mm[s], i)
                nc.scalar.activation(tT[s][:].rearrange("p n c -> p (n c)"), ps[:, 1, :], ACT.Identity, bias=mnb,
                                     scale=mng).then_inc(tT_ready, 1)

            def hid_(i, s):
                act.wait_ge(hid_mm[s], i + 1)
                earlier(act, out_mm[s], i)
                nc.scalar.activation(hid[s][:].rearrange("p n c -> p (n c)"), ps[:, 2, :], ACT.Relu,
                                     bias=b1c).then_inc(hid_ready, 1)

            def zT_(i, s):
                act.wait_ge(zT_mm[s], i + 1)
                nc.scalar.copy(zT[s][:].rearrange("p n c -> p (n c)"), ps[:, 1, :]).then_inc(zT_ready, 1)

            def mask(i, s, n):
                b, k = n % 2, 4 * i + 2 * s + n // 2
                act.wait_ge(oh_ready, 2 * i + s + 1)
                act.wait_ge(ea_mm[b], k + 1)
                earlier(act, add_step[b], 4 * k)
                for e in range(EH):
                    last = nc.scalar.activation(ea[b][:, e], ps[:, 4 + 2 * b, e * F:e * F + F], ACT.Copy,
                                                scale=oh[s][:, n, e:e + 1])
                last.then_inc(ea_done[b], 1)

            def first3():
                root(0, 0, 0)
                tT_(0, 0)
                hid_(0, 0)
                root(0, 0, 1)
                zT_(0, 0)

            def body3(i, s, ahead2, ahead1):
                nxt = after(i, s)
                mask(i, s, 0)
                if ahead1:
                    root(*nxt, 0)
                mask(i, s, 1)
                if ahead1:
                    tT_(*nxt)
                    hid_(*nxt)
                mask(i, s, 2)
                if ahead1:
                    root(*nxt, 1)
                mask(i, s, 3)
                if ahead1:
                    zT_(*nxt)

            two_ahead(act, first3, body3)

        @block.vector
        def _(dve):
            bkvB = bkv[:, :]
            nc.vector.memset(sm[:], 0.0).then_inc(sm_ready[0], 1)
            dve.wait_ge(w_loaded, 16 * 16)
            nc.vector.tensor_copy(bqB[:], bqc.broadcast_to([P, P])).then_inc(bqB_ready, 1)

            def norm_a(s, k, src):
                for n in range(NS):
                    last = nc.vector.bn_stats(st[s][:, n], src(n))
                last.then_inc(stats_done, 1)
                dve.wait_ge(stats_done, k + 1)
                dve.sem_inc(dve_passed, 1)
                for n in range(NS):
                    last = nc.vector.bn_aggr(mv[s][:, n], st[s][:, n])
                last.then_inc(mv_done, 1)
                dve.wait_ge(mv_done, k + 1)
                nc.vector.tensor_scalar(ab[s][:, 0], mv[s][:, :, 1], EPS, None, ALU.add).then_inc(var_done, 1)

            def stats1(i, s):
                norm_a(s, 2 * i + s, lambda n: x_all[:, 2 * i + s, n])
                dve.wait_ge(var_done, 2 * i + s + 1)
                nc.vector.scalar_tensor_tensor(ab[s][:, 1], ab[s][:, 0], EPS, mv[s][:, :, 1], ALU.mult,
                                               ALU.add).then_inc(ab_done, 1)

            def scale1(i, s):
                dve.wait_ge(sd_done, 2 * i + s + 1)
                earlier(dve, h_done[s], i)
                nc.vector.reciprocal(rr[s][:], sd[s][:]).then_inc(rr_done, 1)
                dve.wait_ge(rr_done, 2 * i + s + 1)
                nc.vector.scalar_tensor_tensor(nb[s][:], mv[s][:, :, 0], -1.0, rr[s][:, 0], ALU.mult,
                                               ALU.mult).then_inc(nb_done, 1)
                earlier(dve, xT_mm[s], i)
                for n in range(NS):
                    last = nc.vector.tensor_scalar(xh[s][:, n], x_all[:, 2 * i + s, n], mv[s][:, n, 0:1],
                                                   rr[s][:, 1, n:n + 1], ALU.subtract, ALU.mult)
                last.then_inc(xh_ready, 1)

            def kv1(i, s):
                earlier(dve, kv_kept[s], 16 * i)
                earlier(dve, kT_mm[s], i)
                for n in range(NS):
                    dve.wait_ge(kv_mm[s], NS * i + n + 1)
                    nc.vector.tensor_tensor(kv[s][:, n], ps[:, 1 + n, 0:2 * C], bkvB, ALU.add).then_inc(kv_ready[s], 1)
                nc.vector.tensor_scalar(lr_all[:, bass.ds((2 * i + s) * NS, NS)], ps[:, 1:1 + NS, 2 * C], lrb[:, 0:1], None,
                                        ALU.add).then_inc(lr_ready, 1)

            def k1(i, s):
                dve.wait_ge(sn_done, 2 * i + s + 1)
                nc.vector.reciprocal(rn[s][:], sn[s][:]).then_inc(rn_done[s], 1)
                dve.wait_ge(rn_done[s], i + 1)
                dve.wait_ge(kv_ready[s], NS * (i + 1))
                for n in range(NS):
                    last = nc.vector.tensor_scalar(kv[s][:, n, 0:C], kv[s][:, n, 0:C], rn[s][:, n:n + 1], None, ALU.mult)
                last.then_inc(k_ready, 1)

            def gram1(i, s):
                dve.wait_ge(g_mm[s], i + 1)
                earlier(dve, g_kept[s], 16 * i)
                earlier(dve, gd_done[s], NB * i)
                nc.vector.tensor_copy(gg[s][:].rearrange("p n c -> p (n c)"), ps[:, 6, :]).then_inc(g_ready, 1)

            def first1():
                for s in range(2):
                    dve.wait_ge(x_loaded[s], 16)
                    stats1(0, s)
                    scale1(0, s)
                kv1(0, 0)
                dve.wait_ge(x_rest, 16 * (T - 2))

            def body1(i, s, ahead2, ahead1):
                if ahead2:
                    stats1(i + 1, s)
                k1(i, s)
                if ahead2:
                    scale1(i + 1, s)
                if ahead1:
                    kv1(*after(i, s))
                gram1(i, s)

            two_ahead(dve, first1, body1)

            for s in range(2):
                dve.wait_ge(gd_done[s], NB * NIT)
            nc.vector.transpose(lt[:].rearrange("p c r -> p (c r)"), gd_all[:].rearrange("p c t -> p (c t)")).then_inc(lt_done, 1)
            dve.wait_ge(lt_done, 1)
            dve.wait_ge(xi_ready, 1)
            for j in range(Q - 1):
                m, w = Q - 1 - j, j + 1
                below = prod[:, 0:m * w].rearrange("p (i k) -> p i k", k=w)
                if j:
                    dve.wait_ge(elim, 2 * j)
                nc.vector.tensor_tensor(below, lt[:, j, j + 1:Q].unsqueeze(2).broadcast_to([P, m, w]),
                                        xi[:, j, 0:w].unsqueeze(1).broadcast_to([P, m, w]), ALU.mult).then_inc(elim, 1)
                dve.wait_ge(elim, 2 * j + 1)
                nc.vector.tensor_tensor(xi[:, j + 1:Q, 0:w], xi[:, j + 1:Q, 0:w], below, ALU.subtract).then_inc(elim, 1)
            dve.wait_ge(elim, 2 * (Q - 1))
            nc.vector.transpose(dT_all[:].rearrange("p r t -> p (r t)"), xi[:].rearrange("p r c -> p (r c)")).then_inc(dT_done, 1)
            nc.vector.transpose(d_all[:], xi[:].rearrange("p r c -> p c r")).then_inc(d_done, 1)

            def yb(i, s):
                dve.wait_ge(yb_mm, 2 * i + s + 1)
                earlier(dve, zb_mm[s], i)
                nc.vector.tensor_copy(yT[s][2 * Q:3 * Q].rearrange("p n c -> p (n c)"),
                                      ps[2 * Q:3 * Q, 1, 0:NS * Q]).then_inc(yb_ready, 1)

            def zb(i, s):
                dve.wait_ge(zb_mm[s], i + 1)
                nc.vector.tensor_scalar(tt[s][2 * Q:3 * Q, :, 3 * Q:4 * Q],
                                        ps[2 * Q:3 * Q, 1, NS * Q:2 * NS * Q].rearrange("p (n c) -> p n c", n=NS), -1.0, None,
                                        ALU.mult).then_inc(zb_ready, 1)

            def t12(i, s):
                dve.wait_ge(t12_mm[s], i + 1)
                nc.vector.tensor_scalar(tt[s][0:2 * Q, :, 2 * Q:4 * Q],
                                        ps[0:2 * Q, 2, 2 * NS * Q:4 * NS * Q].rearrange("p (n c) -> p n c", n=NS), -1.0, None,
                                        ALU.mult).then_inc(t12_ready, 1)

            def lru(i, s, n):
                dve.wait_ge(u_ready[n], 2 * i + s + 1)
                nc.vector.tensor_scalar(uu[:, n, C:2 * C], uu[:, n, 0:C], lrs[s][:, n:n + 1], None,
                                        ALU.mult).then_inc(lru_ready[n], 1)

            def add_sm(i, s, n):
                dve.wait_ge(sm_mm[n][s], i + 1)
                nc.vector.tensor_tensor(sm[:, n], ps[:, 6 + n % 2, 0:2 * C], sm[:, n], ALU.add).then_inc(sm_ready[n], 1)

            def first2():
                yb(0, 0)
                zb(0, 0)
                t12(0, 0)

            def body2(i, s, ahead2, ahead1):
                lru(i, s, 0)
                lru(i, s, 1)
                if ahead1:
                    yb(*after(i, s))
                lru(i, s, 2)
                lru(i, s, 3)
                if ahead1:
                    zb(*after(i, s))
                for n in range(NS):
                    add_sm(i, s, n)
                if ahead1:
                    t12(*after(i, s))

            two_ahead(dve, first2, body2)

            dve.wait_ge(fold_mm, 4)
            nc.vector.tensor_tensor(cb[:], tiles(3), bo[:, :].unsqueeze(1).broadcast_to([P, NS, C]), ALU.add).then_inc(cb_ready, 1)

            def norm_b(s, k, src, dst, ready):
                dve.wait_ge(sd_done, k + 1)
                nc.vector.reciprocal(rr[s][:, 0], sd[s][:, 0]).then_inc(rr_done, 1)
                dve.wait_ge(rr_done, k + 1)
                for n in range(NS):
                    last = nc.vector.tensor_scalar(dst[:, n], src[:, n], mv[s][:, n, 0:1], rr[s][:, 0, n:n + 1],
                                                   ALU.subtract, ALU.mult)
                last.then_inc(ready, 1)

            def resid(i, s):
                dve.wait_ge(dl_mm[s], i + 1)
                dve.wait_ge(hcb_ready, 2 * i + s + 1)
                earlier(dve, xb_ready[s], i)
                nc.vector.tensor_tensor(h2[s], tiles(0), hcb[s][:], ALU.add).then_inc(h2_ready[s], 1)
                dve.wait_ge(h2_ready[s], i + 1)
                norm_a(s, norms(i, s, 0), lambda n: h2[s][:, n])

            def tn_(i, s):
                earlier(dve, tT_mm[s], i)
                norm_b(s, norms(i, s, 0), h2[s], tnv[s], tn_ready)

            def mlp_out(i, s):
                dve.wait_ge(out_mm[s], i + 1)
                dve.wait_ge(xb_ready[s], i + 1)
                earlier(dve, xz_ready[s], i)
                nc.vector.tensor_tensor(x1[s], tiles(0), xb[s][:], ALU.add).then_inc(x1_ready[s], 1)
                dve.wait_ge(x1_ready[s], i + 1)
                norm_a(s, norms(i, s, 1), lambda n: x1[s][:, n])

            def z_(i, s):
                earlier(dve, zT_mm[s], i)
                norm_b(s, norms(i, s, 1), x1[s], zv[s], z_ready)

            def choose(i, s):
                def link(ins, k):
                    ins.then_inc(oh_step[s], 1)
                    dve.wait_ge(oh_step[s], 4 * i + k)
                scores = ps[:, 3, 0:NS * E].rearrange("p (n e) -> p n e", n=NS)
                dve.wait_ge(gate_mm, 2 * i + s + 1)
                link(nc.vector.tensor_reduce(mx[s][:], scores, AX_X, ALU.max), 1)
                link(nc.vector.tensor_tensor(eq[s][:], scores, mx[s][:].unsqueeze(2).broadcast_to([P, NS, E]), ALU.is_equal), 2)
                link(nc.vector.tensor_tensor(eq[s][:], eq[s][:], desc[:, :].unsqueeze(1).broadcast_to([P, NS, E]), ALU.mult), 3)
                link(nc.vector.tensor_reduce(m2[s][:], eq[s][:], AX_X, ALU.max), 4)
                nc.vector.tensor_tensor(oh[s][:], eq[s][:], m2[s][:].unsqueeze(2).broadcast_to([P, NS, E]),
                                        ALU.is_equal).then_inc(oh_ready, 1)

            def mask(i, s, n):
                b, k = n % 2, 4 * i + 2 * s + n // 2
                dve.wait_ge(oh_ready, 2 * i + s + 1)
                dve.wait_ge(ed_mm[b], k + 1)
                earlier(dve, add_step[b], 4 * k)
                nc.vector.tensor_tensor(ed[b], ps[:, 5 + 2 * b, :].rearrange("p (e f) -> p e f", e=EH),
                                        oh[s][:, n, EH:E].unsqueeze(2).broadcast_to([P, EH, F]), ALU.mult).then_inc(ed_done[b], 1)

            def first3():
                dve.wait_ge(consts_ready, E + 4)
                resid(0, 0)
                tn_(0, 0)
                mlp_out(0, 0)
                z_(0, 0)
                choose(0, 0)

            def body3(i, s, ahead2, ahead1):
                nxt = after(i, s)
                if ahead1:
                    resid(*nxt)
                mask(i, s, 0)
                if ahead1:
                    tn_(*nxt)
                mask(i, s, 1)
                mask(i, s, 2)
                if ahead1:
                    mlp_out(*nxt)
                    z_(*nxt)
                mask(i, s, 3)
                if ahead1:
                    choose(*nxt)

            two_ahead(dve, first3, body3)

        @block.tensor
        def _(pe):
            pe.wait_ge(id_ready, 1)
            pe.wait_ge(w_loaded, 16 * 16)

            def four(bank, lhsT, rhs, ready, step=1):
                for n in range(NS):
                    last = nc.tensor.matmul(tiles(bank)[:, n], lhsT(n), rhs(n), start=True, stop=True)
                last.then_inc(ready, step)

            def turn(bank, src, ready):
                for n in range(NS):
                    last = nc.tensor.transpose(tiles(bank)[:, n], src(n), ident[:])
                last.then_inc(ready, 1)

            def xT1(i, s):
                pe.wait_ge(xh_ready, 2 * i + s + 1)
                earlier(pe, xnT_ready, 2 * i + s)
                turn(0, lambda n: xh[s][:, n], xT_mm[s])

            def kvm1(i, s):
                pe.wait_ge(xnT_ready, 2 * i + s + 1)
                earlier(pe, lr_ready, 2 * i + s)
                for n in range(NS):
                    nc.tensor.matmul(ps[:, 1 + n, 0:KVW], xnT[s][:, n * P:n * P + P], wkvl[:], start=True,
                                     stop=True).then_inc(kv_mm[s], 1)

            def kT1(i, s):
                pe.wait_ge(k_ready, 2 * i + s + 1)
                earlier(pe, kT_ready, 2 * i + s)
                turn(5, lambda n: kv[s][:, n, 0:C], kT_mm[s])

            def gram1(i, s):
                pe.wait_ge(kT_ready, 2 * i + s + 1)
                earlier(pe, g_ready, 2 * i + s)
                four(6, lambda n: kT[s][:, n * P:n * P + P], lambda n: kT[s][:, n * P:n * P + P], g_mm[s])

            def first1():
                xT1(0, 0)
                kvm1(0, 0)

            def body1(i, s, ahead2, ahead1):
                if ahead1:
                    xT1(*after(i, s))
                kT1(i, s)
                if ahead1:
                    kvm1(*after(i, s))
                gram1(i, s)

            two_ahead(pe, first1, body1)

            pe.wait_ge(xnT_ready, T)
            pe.wait_ge(lr_ready, T)
            pe.wait_ge(e_loaded, 32)
            nc.tensor.transpose(ps[:, 0, 0:C], wq[:], ident[:])
            nc.tensor.transpose(ps[:, 0, C:C + E], gw[:], ident[0:E, 0:E]).then_inc(wqT_mm, 1)
            for q in range(2):
                turn(1 + q, lambda n: ew[:, EH * q + n], ewT_mm)

            pe.wait_ge(wqT_ready, 1)
            pe.wait_ge(ewT_ready, 1)
            pe.wait_ge(kT_ready, T)
            pe.wait_ge(g_ready, T)

            def ya(i, s):
                pe.wait_ge(blocks_set, SET * (2 * i + s + 1))
                pe.wait_ge(gs_loaded[s], 16 * (i + 1))
                earlier(pe, za_ready, 2 * i + s)
                earlier(pe, zb_ready, 2 * i + s)
                pe.sem_inc(pe_passed, 1)
                for bank, lo, ready in ((0, 0, ya_mm), (1, 2 * Q, yb_mm)):
                    hi = lo + Q
                    for n in range(NS):
                        last = nc.tensor.matmul(ps[lo:lo + Q, bank, n * Q:n * Q + Q], gs[s][hi:hi + Q, n, lo:lo + Q],
                                                tt[s][hi:hi + Q, n, hi:hi + Q], start=True, stop=True)
                    last.then_inc(ready, 1)

            def za(i, s):
                pe.wait_ge(ya_ready, 2 * i + s + 1)
                pe.sem_inc(pe_passed, 1)
                for n in range(NS):
                    nc.tensor.matmul(ps[0:Q, 0, (NS + n) * Q:(NS + n + 1) * Q], da[s][0:Q, n, 0:Q], yT[s][0:Q, n],
                                     start=True, stop=True)
                for n in range(NS):
                    last = nc.tensor.matmul(ps[Q:2 * Q, 0, (2 * NS + n) * Q:(2 * NS + n + 1) * Q], yT[s][0:Q, n],
                                            da[s][0:Q, n, 0:Q], start=True, stop=True)
                last.then_inc(za_mm[s], 1)
                pe.wait_ge(yb_ready, 2 * i + s + 1)
                pe.sem_inc(pe_passed, 1)
                for n in range(NS):
                    last = nc.tensor.matmul(ps[2 * Q:3 * Q, 1, (NS + n) * Q:(NS + n + 1) * Q], da[s][2 * Q:3 * Q, n, 0:Q],
                                            yT[s][2 * Q:3 * Q, n], start=True, stop=True)
                last.then_inc(zb_mm[s], 1)

            def y64_(i, s):
                pe.wait_ge(zb_ready, 2 * i + s + 1)
                earlier(pe, t12_ready, 2 * i + s)
                pe.sem_inc(pe_passed, 1)
                for n in range(NS):
                    last = nc.tensor.matmul(ps[0:2 * Q, 2, 2 * n * Q:2 * (n + 1) * Q], gs[s][2 * Q:4 * Q, n, 0:2 * Q],
                                            tt[s][2 * Q:4 * Q, n, 2 * Q:4 * Q], start=True, stop=True)
                last.then_inc(y64_mm[s], 1)

            def t12(i, s):
                pe.wait_ge(y64_ready, 2 * i + s + 1)
                pe.wait_ge(za_ready, 2 * i + s + 1)
                pe.sem_inc(pe_passed, 1)
                for n in range(NS):
                    last = nc.tensor.matmul(ps[0:2 * Q, 2, 2 * (NS + n) * Q:2 * (NS + n + 1) * Q], da[s][0:2 * Q, n, :],
                                            y64[s][:, n], start=True, stop=True)
                last.then_inc(t12_mm[s], 1)

            def uw(i, s):
                pe.wait_ge(t12_ready, 2 * i + s + 1)
                pe.wait_ge(kvs_loaded[s], 16 * (i + 1))
                earlier(pe, u_ready[2], 2 * i + s)
                earlier(pe, u_ready[3], 2 * i + s)
                for n in range(NS):
                    nc.tensor.matmul(tiles(3 + n % 2)[:, n], tt[s][:, n], kvs[s][:, n, C:2 * C], start=n < 2, stop=False,
                                     skip_group_check=True)
                earlier(pe, wT_ready, 2 * i + s)
                four(5, lambda n: kvs[s][:, n, 0:C], lambda n: tt[s][:, n], wT_mm[s])

            def u_(i, s, n):
                if n == 0:
                    pe.wait_ge(wT_ready, 2 * i + s + 1)
                if n >= 2:
                    pe.wait_ge(u_ready[n - 2], 2 * i + s + 1)
                earlier(pe, sm_ready[n], 2 * i + s + (1 if n == 0 else 0))
                nc.tensor.matmul(tiles(3 + n % 2)[:, n], wT[s][:, n], sm[:, n, 0:C], start=False, stop=True,
                                 skip_group_check=True).then_inc(u_mm[n], 1)

            def sm_(i, s, n):
                pe.wait_ge(lru_ready[n], 2 * i + s + 1)
                if n >= 2:
                    pe.wait_ge(sm_ready[n - 2], 2 * i + s + (2 if n == 2 else 1))
                nc.tensor.matmul(ps[:, 6 + n % 2, 0:2 * C], kvs[s][:, n, 0:C], uu[:, n], start=True,
                                 stop=True).then_inc(sm_mm[n][s], 1)

            def first2():
                ya(0, 0)
                za(0, 0)
                y64_(0, 0)
                t12(0, 0)
                uw(0, 0)
                pe.wait_ge(sm_ready[0], 1)

            def body2(i, s, ahead2, ahead1):
                nxt = after(i, s)
                u_(i, s, 0)
                u_(i, s, 1)
                if ahead1:
                    ya(*nxt)
                u_(i, s, 2)
                u_(i, s, 3)
                if ahead1:
                    za(*nxt)
                sm_(i, s, 0)
                sm_(i, s, 1)
                if ahead1:
                    y64_(*nxt)
                sm_(i, s, 2)
                sm_(i, s, 3)
                if ahead1:
                    t12(*nxt)
                    uw(*nxt)

            two_ahead(pe, first2, body2)

            for n in range(NS):
                pe.wait_ge(sm_ready[n], T + (1 if n == 0 else 0))
            turn(0, lambda n: sm[:, n, C:2 * C], fold_mm)
            pe.wait_ge(fold_out, 1)
            four(1, lambda n: mT[:, n * C:n * C + C], lambda n: wo[:], fold_mm)
            pe.wait_ge(fold_out, 2)
            nc.tensor.matmul(ps[:, 2, :], wqT[:], mw[:], start=True, stop=True).then_inc(fold_mm, 1)
            pe.wait_ge(bqB_ready, 1)
            nc.tensor.matmul(ps[:, 3, :], bqB[:], mw[:], start=True, stop=True).then_inc(fold_mm, 1)
            pe.wait_ge(fold_out, 3)
            pe.wait_ge(cb_ready, 1)

            def delta(i, s):
                pe.wait_ge(xns_loaded[s], 16 * (i + 1))
                earlier(pe, x1_ready[1 - s], i + s)
                four(0, lambda n: xns[s][:, n], lambda n: gn[:, n], dl_mm[s])

            def tT_(i, s):
                pe.wait_ge(tn_ready, 2 * i + s + 1)
                earlier(pe, zT_ready, 2 * i + s)
                turn(1, lambda n: tnv[s][:, n], tT_mm[s])

            def hid_(i, s):
                pe.wait_ge(tT_ready, 2 * i + s + 1)
                earlier(pe, hid_ready, 2 * i + s)
                nc.tensor.matmul(ps[:, 2, :], w1s[:], tT[s][:].rearrange("p n c -> p (n c)"), start=True,
                                 stop=True).then_inc(hid_mm[s], 1)

            def out_(i, s):
                pe.wait_ge(hid_ready, 2 * i + s + 1)
                pe.wait_ge(h2_ready[s], i + 1)
                four(0, lambda n: hid[s][:, n], lambda n: w2s[:], out_mm[s])

            def zT_(i, s):
                pe.wait_ge(z_ready, 2 * i + s + 1)
                pe.wait_ge(tT_ready, 2 * i + s + 1)
                turn(1, lambda n: zv[s][:, n], zT_mm[s])

            def gate(i, s):
                pe.wait_ge(zT_ready, 2 * i + s + 1)
                earlier(pe, oh_ready, 2 * i + s)
                for n in range(NS):
                    last = nc.tensor.matmul(ps[:, 3, n * E:n * E + E], zT[s][:, n], gwT[:], start=True, stop=True)
                last.then_inc(gate_mm, 1)

            def experts(i, s, n):
                b, k = n % 2, 4 * i + 2 * s + n // 2
                for half, bank, used, ready in ((0, 4 + 2 * b, ea_done, ea_mm), (1, 5 + 2 * b, ed_done, ed_mm)):
                    earlier(pe, used[b], k)
                    nc.tensor.matmul(ps[:, bank, :], zT[s][:, n],
                                     ewT[:, EH * half:EH * half + EH, :].rearrange("p e f -> p (e f)"), start=True,
                                     stop=True).then_inc(ready[b], 1)

            def first3():
                delta(0, 0)
                tT_(0, 0)
                hid_(0, 0)
                out_(0, 0)
                zT_(0, 0)
                gate(0, 0)

            def body3(i, s, ahead2, ahead1):
                nxt = after(i, s)
                if ahead1:
                    delta(*nxt)
                experts(i, s, 0)
                if ahead1:
                    tT_(*nxt)
                experts(i, s, 1)
                if ahead1:
                    hid_(*nxt)
                experts(i, s, 2)
                if ahead1:
                    out_(*nxt)
                experts(i, s, 3)
                if ahead1:
                    zT_(*nxt)
                    gate(*nxt)

            two_ahead(pe, first3, body3)


_INS = ["x", "dn_g", "dn_b", "gates_w", "gates_b", "lr_w", "lr_b", "out_w", "out_b", "mn_g", "mn_b", "w1", "b1", "w2", "b2"]


def kernel(**inputs):
    import numpy as _np
    import concourse.bacc as _bacc
    from concourse import mybir as _mybir
    from concourse.bass_utils import run_bass_kernel_spmd as _run

    nc = _bacc.Bacc("TRN2", target_bir_lowering=False, num_devices=1)
    arrays, args = {}, []
    for name in [f"L0_attn_{n}" for n in _INS] + ["L0_ffn_gate_w", "L0_ffn_expert_w"]:
        a = _np.ascontiguousarray(inputs[name])
        arrays[f"in_{name}_dram"] = a
        args.append(nc.dram_tensor(f"in_{name}_dram", a.shape, _mybir.dt.from_np(a.dtype), kind="ExternalInput").ap())
    shape = inputs["L0_attn_x"].shape
    args.append(nc.dram_tensor("out_dram", shape, _mybir.dt.float32, kind="ExternalOutput").ap())
    delta_block_kernel(nc, *args)
    r = _run(nc, [arrays], core_ids=[0])
    return r.results[0]["out_dram"]
```

```python
from contextlib import ExitStack

import concourse.bass as bass
from concourse import mybir

P = 128
Q = 32
EPS = 1e-5

ALU = mybir.AluOpType
ACT = mybir.ActivationFunctionType
AX_X = mybir.AxisListType.X
F32 = mybir.dt.float32


def delta_block_kernel(
    nc: bass.Bass,
    x: bass.AP, dn_g: bass.AP, dn_b: bass.AP, gates_w: bass.AP, gates_b: bass.AP,
    lr_w: bass.AP, lr_b: bass.AP, out_w: bass.AP, out_b: bass.AP,
    mn_g: bass.AP, mn_b: bass.AP, w1: bass.AP, b1: bass.AP, w2: bass.AP, b2: bass.AP,
    gate_w: bass.AP, expert_w: bass.AP,
    out: bass.AP,
):
    NS, L, C = x.shape
    E, F, _ = expert_w.shape
    T = L // P
    NIT = T // 2
    NB = P // Q
    TN = T * NS
    KVW = 2 * C + 1
    EH = E // 2
    ADDS = 3
    assert C == P and F == P and NS == 4 and TN == Q and E == 8 and T % 2 == 0

    x_v = x.rearrange("n (t p) c -> p t n c", p=P)
    out_v = out.rearrange("n (t p) c -> p t n c", p=P)

    with ExitStack() as ctx:
        def sb(name, shape):
            return ctx.enter_context(nc.sbuf_tensor(name, shape, F32))

        def sem(name):
            return ctx.enter_context(nc.semaphore(name))

        def pair(name):
            return [sem(f"{name}{s}") for s in range(2)]

        def each(name):
            return [sem(f"{name}{n}") for n in range(NS)]

        ps = ctx.enter_context(nc.psum_tensor("ps", [P, 8, 512], F32))

        def tiles(bank, width=P):
            return ps[:, bank, 0:NS * width].rearrange("p (n c) -> p n c", n=NS)

        ident = sb("ident", [P, P])
        desc = sb("desc", [P, E])
        wq = sb("wq", [P, C])
        wqT = sb("wqT", [P, C])
        wkvl = sb("wkvl", [P, KVW])
        bkv = sb("bkv", [P, 2 * C])
        lrb = sb("lrb", [P, 1])
        wo = sb("wo", [P, C])
        bo = sb("bo", [P, C])
        w1s = sb("w1s", [P, C])
        w2s = sb("w2s", [P, C])
        b2s = sb("b2s", [P, C])
        cols = sb("cols", [P, 6])
        dng, dnb, mng, mnb, b1c, bqc = [cols[:, j:j + 1] for j in range(6)]
        bqB = sb("bqB", [P, P])
        gw = sb("gw", [E, C])
        gwT = sb("gwT", [P, E])
        ew = sb("ew", [P, E, C])
        ewT = sb("ewT", [P, E, F])

        x_all = sb("x_all", [P, T, NS, C])
        h_all = sb("h_all", [P, T, NS, C])
        xnT_all = sb("xnT_all", [P, T, NS * P])
        kv_all = sb("kv_all", [P, T, NS * 2 * C])
        g_all = sb("g_all", [P, T, NS * P])
        lr_all = sb("lr_all", [P, TN])
        gd_all = sb("gd_all", [P, Q, TN])
        lt = sb("lt", [P, Q, Q])
        xi = sb("xi", [P, Q, Q])
        prod = sb("prod", [P, Q * Q])
        dT_all = sb("dT_all", [P, Q, TN])
        d_all = sb("d_all", [P, Q, TN])

        st = [sb(f"st{s}", [P, NS, 6]) for s in range(2)]
        mv = [sb(f"mv{s}", [P, NS, 2]) for s in range(2)]
        ab = [sb(f"ab{s}", [P, 2, NS]) for s in range(2)]
        sd = [sb(f"sd{s}", [P, 2, NS]) for s in range(2)]
        rr = [sb(f"rr{s}", [P, 2, NS]) for s in range(2)]
        nb = [sb(f"nb{s}", [P, NS]) for s in range(2)]
        xh = [sb(f"xh{s}", [P, NS, C]) for s in range(2)]
        xnT = [sb(f"xnT{s}", [P, NS * P]) for s in range(2)]
        kv = [sb(f"kv{s}", [P, NS, 2 * C]) for s in range(2)]
        sq = sb("sq", [P, NS, C])
        ss = [sb(f"ss{s}", [P, NS]) for s in range(2)]
        sn = [sb(f"sn{s}", [P, NS]) for s in range(2)]
        rn = [sb(f"rn{s}", [P, NS]) for s in range(2)]
        kT = [sb(f"kT{s}", [P, NS * P]) for s in range(2)]
        gg = [sb(f"gg{s}", [P, NS, P]) for s in range(2)]

        kvs = [sb(f"kvs{s}", [P, NS, 2 * C]) for s in range(2)]
        gs = [sb(f"gs{s}", [P, NS, P]) for s in range(2)]
        tt = [sb(f"tt{s}", [P, NS, P]) for s in range(2)]
        da = [sb(f"da{s}", [P, NS, 2 * Q]) for s in range(2)]
        yT = [sb(f"yT{s}", [P, NS, Q]) for s in range(2)]
        y64 = [sb(f"y64{s}", [2 * Q, NS, 2 * Q]) for s in range(2)]
        wT = [sb(f"wT{s}", [P, NS, P]) for s in range(2)]
        uu = sb("uu", [P, NS, 2 * C])
        sm = sb("sm", [P, NS, 2 * C])

        mT = sb("mT", [P, NS * C])
        mw = sb("mw", [P, NS * C])
        gn = sb("gn", [P, NS, C])
        cb = sb("cb", [P, NS, C])

        xns = [sb(f"xns{s}", [P, NS, P]) for s in range(2)]
        tn, z = xnT, kT
        tnv = [t[:, :].rearrange("p (n c) -> p n c", n=NS) for t in tn]
        zv = [t[:, :].rearrange("p (n c) -> p n c", n=NS) for t in z]
        tT = gg
        hid = wT
        zT = tt
        mx = [sb(f"mx{s}", [P, NS]) for s in range(2)]
        eq = [sb(f"eq{s}", [P, NS, E]) for s in range(2)]
        m2 = [sb(f"m2{s}", [P, NS]) for s in range(2)]
        oh = [sb(f"oh{s}", [P, NS, E]) for s in range(2)]
        ea, ed, es = [[t[:, :, :].rearrange("p a b -> p (a b)")[:, b * EH * F:(b + 1) * EH * F].rearrange("p (e f) -> p e f", e=EH)
                       for b in range(2)] for t in (gd_all, lt, xi)]

        x_loaded, x_rest, e_loaded = pair("x_loaded"), sem("x_rest"), sem("e_loaded")
        kvw_loaded, w_loaded = sem("kvw_loaded"), sem("w_loaded")
        id_zero, id_ready, consts_ready = sem("id_zero"), sem("id_ready"), sem("consts_ready")
        bqB_ready, wqT_mm, wqT_ready = sem("bqB_ready"), sem("wqT_mm"), sem("wqT_ready")
        stats_done, mv_done, var_done, ab_done = sem("stats_done"), sem("mv_done"), sem("var_done"), sem("ab_done")
        sd_done, rr_done, nb_done, h_done = sem("sd_done"), sem("rr_done"), sem("nb_done"), pair("h_done")
        xh_ready, xT_mm, xnT_ready, xnT_kept = sem("xh_ready"), pair("xT_mm"), sem("xnT_ready"), pair("xnT_kept")
        kv_mm, kv_ready, lr_ready = pair("kv_mm"), pair("kv_ready"), sem("lr_ready")
        ss_done, sn_done, rn_done, k_ready, kv_kept = (sem("ss_done"), sem("sn_done"), pair("rn_done"),
                                                       sem("k_ready"), pair("kv_kept"))
        kT_mm, kT_ready, g_mm, g_ready, g_kept, gd_done = (pair("kT_mm"), sem("kT_ready"), pair("g_mm"),
                                                           sem("g_ready"), pair("g_kept"), pair("gd_done"))
        xi_ready, lt_done, elim, dT_done, d_done = (sem("xi_ready"), sem("lt_done"), sem("elim"), sem("dT_done"),
                                                    sem("d_done"))
        ewT_mm, ewT_ready, gwT_ready = sem("ewT_mm"), sem("ewT_ready"), sem("gwT_ready")
        kvs_loaded, gs_loaded = pair("kvs_loaded"), pair("gs_loaded")
        tt_set, da_set = sem("tt_set"), sem("da_set")
        ya_mm, yb_mm, ya_ready, yb_ready = sem("ya_mm"), sem("yb_mm"), sem("ya_ready"), sem("yb_ready")
        za_mm, zb_mm, za_ready, zb_ready = pair("za_mm"), pair("zb_mm"), sem("za_ready"), sem("zb_ready")
        y64_mm, y64_ready, t12_mm, t12_ready = pair("y64_mm"), sem("y64_ready"), pair("t12_mm"), sem("t12_ready")
        wT_mm, wT_ready = pair("wT_mm"), sem("wT_ready")
        u_mm, u_ready, lru_ready, sm_ready = each("u_mm"), each("u_ready"), each("lru_ready"), each("sm_ready")
        sm_mm = [pair(f"sm_mm{n}_") for n in range(NS)]
        fold_mm, fold_out, cb_ready = sem("fold_mm"), sem("fold_out"), sem("cb_ready")
        xns_loaded, dl_mm, hcb_ready, h2_ready = pair("xns_loaded"), pair("dl_mm"), sem("hcb_ready"), pair("h2_ready")
        tn_ready, tT_mm, tT_ready, xb_ready = sem("tn_ready"), pair("tT_mm"), sem("tT_ready"), pair("xb_ready")
        hid_mm, hid_ready, out_mm, x1_ready = pair("hid_mm"), sem("hid_ready"), pair("out_mm"), pair("x1_ready")
        z_ready, zT_mm, zT_ready, ewI_ready = sem("z_ready"), pair("zT_mm"), sem("zT_ready"), sem("ewI_ready")
        gate_mm, oh_step, oh_ready = sem("gate_mm"), pair("oh_step"), sem("oh_ready")
        ea_mm, ed_mm, ea_done, ed_done, sum_done = (pair("ea_mm"), pair("ed_mm"), pair("ea_done"), pair("ed_done"),
                                                     pair("sum_done"))
        add_step, stored = pair("add_step"), sem("stored")

        dve_passed, pe_passed = sem("dve_passed"), sem("pe_passed")

        block = ctx.enter_context(nc.Block())

        def earlier(eng, semaphore, value):
            if not isinstance(value, int) or value > 0:
                eng.wait_ge(semaphore, value)

        def norms(i, s, second):
            return T + 2 * (2 * i + s) + second

        def after(i, s):
            return (i, 1) if s == 0 else (i + 1, 0)

        def two_ahead(eng, first, body):
            first()
            body(0, 0, True, True)
            body(0, 1, True, True)
            with eng.Fori(1, NIT - 1) as i:
                body(i, 0, True, True)
                body(i, 1, True, True)
            body(NIT - 1, 0, False, True)
            body(NIT - 1, 1, False, False)

        def in_turn(eng, body):
            body(0, 0)
            body(0, 1)
            with eng.Fori(1, NIT) as i:
                body(i, 0)
                body(i, 1)

        @block.sync
        def _(sp):
            sp.dma_start(x_all[:, 0], x_v[:, 0]).then_inc(x_loaded[0], 16)
            for dst, src in ((dng, dn_g.unsqueeze(1)), (dnb, dn_b.unsqueeze(1)), (wkvl[:, 0:2 * C], gates_w[:, C:3 * C]),
                             (wkvl[:, 2 * C:KVW], lr_w), (bkv[:, :], gates_b[C:3 * C].partition_broadcast(P)),
                             (lrb[:, :], lr_b.partition_broadcast(P))):
                sp.dma_start(dst, src).then_inc(kvw_loaded, 16)
            for t in range(1, T):
                sp.dma_start(x_all[:, t], x_v[:, t]).then_inc(x_loaded[1] if t == 1 else x_rest, 16)
            for dst, src in ((b2s[:, :], b2.partition_broadcast(P)), (wq[:, :], gates_w[:, 0:C]), (wo[:, :], out_w),
                             (w1s[:, :], w1), (w2s[:, :], w2), (bo[:, :], out_b.partition_broadcast(P)),
                             (mng, mn_g.unsqueeze(1)), (mnb, mn_b.unsqueeze(1)), (b1c, b1.unsqueeze(1)),
                             (bqc, gates_b[0:C].unsqueeze(1))):
                sp.dma_start(dst, src).then_inc(w_loaded, 16)
            sp.dma_start(gw[:, :], gate_w).then_inc(e_loaded, 16)
            sp.dma_start(ew[:, :, :], expert_w.rearrange("e f h -> f e h")).then_inc(e_loaded, 16)

            def keep_xn(i, s):
                sp.wait_ge(x_loaded[0], 16)
                sp.wait_ge(xnT_ready, 2 * i + s + 1)
                sp.dma_start(xnT_all[:, 2 * i + s, :], xnT[s][:, :]).then_inc(xnT_kept[s], 16)

            def keep_kv(i, s):
                sp.wait_ge(x_loaded[0], 16)
                sp.wait_ge(k_ready, 2 * i + s + 1)
                sp.dma_start(kv_all[:, 2 * i + s, :], kv[s][:, :, :].rearrange("p n c -> p (n c)")).then_inc(kv_kept[s], 16)

            def keep_g(i, s):
                sp.wait_ge(x_loaded[0], 16)
                sp.wait_ge(g_ready, 2 * i + s + 1)
                sp.dma_start(g_all[:, 2 * i + s, :], gg[s][:, :, :].rearrange("p n c -> p (n c)")).then_inc(g_kept[s], 16)

            def first1():
                keep_xn(0, 0)
                keep_xn(0, 1)

            def body1(i, s, ahead2, ahead1):
                nxt = after(i, s)
                keep_kv(i, s)
                if ahead2:
                    keep_xn(i + 1, s)
                keep_g(i, s)

            two_ahead(sp, first1, body1)

            for s in range(2):
                sp.wait_ge(kv_kept[s], 16 * NIT)
                sp.wait_ge(g_kept[s], 16 * NIT)
                sp.wait_ge(xnT_kept[s], 16 * NIT)

            def stage_g(i, s):
                sp.wait_ge(x_loaded[0], 16)
                earlier(sp, y64_mm[s], i)
                sp.dma_start(gs[s][:, :, :].rearrange("p n c -> p (n c)"), g_all[:, 2 * i + s, :]).then_inc(gs_loaded[s], 16)

            def stage_kv(i, s):
                sp.wait_ge(x_loaded[0], 16)
                earlier(sp, sm_mm[NS - 1][s], i)
                sp.dma_start(kvs[s][:, :, :].rearrange("p n c -> p (n c)"), kv_all[:, 2 * i + s, :]).then_inc(kvs_loaded[s], 16)

            def first2():
                stage_g(0, 0)
                stage_kv(0, 0)
                stage_g(0, 1)

            def body2(i, s, ahead2, ahead1):
                nxt = after(i, s)
                if ahead2:
                    stage_g(i + 1, s)
                if ahead1:
                    stage_kv(*nxt)

            two_ahead(sp, first2, body2)

            def stage3(i, s):
                sp.wait_ge(x_loaded[0], 16)
                earlier(sp, dl_mm[s], i)
                sp.dma_start(xns[s][:, :, :].rearrange("p n c -> p (n c)"), xnT_all[:, 2 * i + s, :]).then_inc(xns_loaded[s], 16)

            def store(i, s):
                sp.wait_ge(x_loaded[0], 16)
                for b in range(2):
                    sp.wait_ge(add_step[b], ADDS * (4 * i + 2 * s + 2))
                sp.dma_start(out_v[:, 2 * i + s], x_all[:, 2 * i + s]).then_inc(stored, 16)

            stage3(0, 0)
            stage3(0, 1)
            stage3(1, 0)
            stage3(1, 1)
            store(0, 0)
            with sp.Fori(1, NIT - 1) as i:
                stage3(i + 1, 0)
                store(i - 1, 1)
                stage3(i + 1, 1)
                store(i, 0)
            store(NIT - 2, 1)
            store(NIT - 1, 0)
            store(NIT - 1, 1)
            sp.wait_ge(stored, 16 * T)

        @block.gpsimd
        def _(pool):
            nc.gpsimd.memset(ident[:], 0.0).then_inc(id_zero, 1)
            nc.gpsimd.memset(xi[:], 0.0).then_inc(id_zero, 1)
            pool.wait_ge(id_zero, 2)
            nc.gpsimd.affine_select(out=ident[:], in_=ident[:], compare_op=ALU.not_equal, fill=1.0, base=0,
                                    pattern=[[-1, P]], channel_multiplier=1).then_inc(id_ready, 1)
            nc.gpsimd.affine_select(out=xi[:], in_=xi[:], compare_op=ALU.not_equal, fill=1.0, base=0,
                                    pattern=[[1, Q], [-1, Q]], channel_multiplier=0).then_inc(xi_ready, 1)
            for e in range(E):
                nc.gpsimd.memset(desc[:, e:e + 1], float(E - e)).then_inc(consts_ready, 1)
            for s in range(2):
                nc.gpsimd.memset(tt[s][:], 0.0).then_inc(consts_ready, 1)
                nc.gpsimd.memset(da[s][:], 0.0).then_inc(consts_ready, 1)

            pool.wait_ge(xi_ready, 1)
            pool.wait_ge(consts_ready, E + 4)

            pool.wait_ge(w_loaded, 16 * 10)
            b2B = b2s[:, :].unsqueeze(1).broadcast_to([P, NS, C])

            def diagonals(i, s):
                pool.wait_ge(g_ready, 2 * i + s + 1)
                for b in range(NB):
                    r = slice(Q * b, Q * b + Q)
                    nc.gpsimd.tensor_copy(
                        gd_all[r, :, bass.ds((2 * i + s) * NS, NS)].rearrange("p c n -> p n c"),
                        gg[s][r, :, Q * b:Q * b + Q]).then_inc(gd_done[s], 1)
                    pool.wait_ge(gd_done[s], NB * i + b + 1)

            def plus_b2(i, s):
                pool.wait_ge(h_done[s], i + 1)
                nc.gpsimd.tensor_tensor(x_all[:, 2 * i + s], x_all[:, 2 * i + s], b2B, ALU.add)

            def both(i, s):
                diagonals(i, s)
                plus_b2(i, s)

            both(0, 0)
            both(0, 1)
            with pool.Fori(1, NIT - 1) as i:
                both(i, 0)
                both(i, 1)
            both(NIT - 1, 0)
            plus_b2(NIT - 1, 1)

            pool.wait_ge(ewT_ready, 1)
            nc.gpsimd.tensor_tensor(ewT[:], ewT[:], ident[:, :].unsqueeze(1).broadcast_to([P, E, F]), ALU.add).then_inc(ewI_ready, 1)

            pool.wait_ge(cb_ready, 1)

            def hcb_(i, s):
                nc.gpsimd.tensor_tensor(h_all[:, 2 * i + s], h_all[:, 2 * i + s], cb[:], ALU.add).then_inc(hcb_ready, 1)

            def xb_(i, s):
                pool.wait_ge(h2_ready[s], i + 1)
                nc.gpsimd.tensor_tensor(x_all[:, 2 * i + s], x_all[:, 2 * i + s], h_all[:, 2 * i + s], ALU.add).then_inc(xb_ready[s], 1)

            def total(i, s, n):
                b, k = n % 2, 4 * i + 2 * s + n // 2
                pool.wait_ge(sum_done[b], k + 1)
                nc.gpsimd.tensor_tensor(es[b][:, 0:2], es[b][:, 0:2], es[b][:, 2:4], ALU.add).then_inc(add_step[b], 1)
                pool.wait_ge(add_step[b], ADDS * k + 1)
                nc.gpsimd.tensor_tensor(es[b][:, 0], es[b][:, 0], es[b][:, 1], ALU.add).then_inc(add_step[b], 1)
                pool.wait_ge(add_step[b], ADDS * k + 2)
                nc.gpsimd.tensor_tensor(x_all[:, 2 * i + s, n], es[b][:, 0], x_all[:, 2 * i + s, n], ALU.add).then_inc(add_step[b], 1)

            def first3():
                hcb_(0, 0)
                xb_(0, 0)
                hcb_(0, 1)
                xb_(0, 1)

            def body3(i, s, ahead2, ahead1):
                nxt = after(i, s)
                if ahead2:
                    hcb_(i + 1, s)
                    xb_(i + 1, s)
                total(i, s, 0)
                total(i, s, 1)
                total(i, s, 2)
                total(i, s, 3)

            two_ahead(pool, first3, body3)

        @block.scalar
        def _(act):
            def roots1(i, s):
                act.wait_ge(ab_done, 2 * i + s + 1)
                nc.scalar.activation(sd[s][:], ab[s][:], ACT.Sqrt).then_inc(sd_done, 1)

            def h1(i, s):
                act.wait_ge(nb_done, 2 * i + s + 1)
                for n in range(NS):
                    last = nc.scalar.activation(h_all[:, 2 * i + s, n], x_all[:, 2 * i + s, n], ACT.Identity,
                                                bias=nb[s][:, n:n + 1], scale=rr[s][:, 0, n:n + 1])
                last.then_inc(h_done[s], 1)

            def xn1(i, s):
                act.wait_ge(xT_mm[s], i + 1)
                earlier(act, kv_mm[s], NS * i)
                earlier(act, xnT_kept[s], 16 * i)
                nc.scalar.activation(xnT[s][:], ps[:, 0, :], ACT.Identity, bias=dnb, scale=dng).then_inc(xnT_ready, 1)

            def norms1(i, s):
                earlier(act, rn_done[s], i)
                for n in range(NS):
                    act.wait_ge(kv_ready[s], NS * i + n + 1)
                    last = nc.scalar.activation(sq[:, n], kv[s][:, n, 0:C], ACT.Square, accum_out=ss[s][:, n:n + 1])
                last.then_inc(ss_done, 1)
                act.wait_ge(ss_done, 2 * i + s + 1)
                nc.scalar.activation(sn[s][:], ss[s][:], ACT.Sqrt).then_inc(sn_done, 1)

            def kT1(i, s):
                act.wait_ge(kT_mm[s], i + 1)
                earlier(act, g_mm[s], i)
                nc.scalar.copy(kT[s][:], ps[:, 5, :]).then_inc(kT_ready, 1)

            def gram1(i, s):
                act.wait_ge(g_mm[s], i + 1)
                earlier(act, g_kept[s], 16 * i)
                earlier(act, gd_done[s], NB * i)
                nc.scalar.copy(gg[s][:].rearrange("p n c -> p (n c)"), ps[:, 6, :]).then_inc(g_ready, 1)

            def first1():
                roots1(0, 0)
                act.wait_ge(kvw_loaded, 16 * 6)
                xn1(0, 0)
                roots1(0, 1)
                h1(0, 0)
                xn1(0, 1)
                norms1(0, 0)

            def body1(i, s, ahead2, ahead1):
                nxt = after(i, s)
                if ahead2:
                    roots1(i + 1, s)
                if ahead1:
                    h1(*nxt)
                kT1(i, s)
                if ahead2:
                    xn1(i + 1, s)
                if ahead1:
                    norms1(*nxt)
                gram1(i, s)

            two_ahead(act, first1, body1)

            act.wait_ge(g_ready, T)
            for b in range(NB):
                r = slice(Q * b, Q * b + Q)
                nc.scalar.copy(gd_all[r, :, (T - 1) * NS:T * NS].rearrange("p c n -> p n c"),
                               gg[1][r, :, Q * b:Q * b + Q]).then_inc(gd_done[1], 1)
            act.wait_ge(w_loaded, 16 * 10)

            act.wait_ge(wqT_mm, 1)
            nc.scalar.copy(wqT[:], ps[:, 0, 0:C])
            nc.scalar.copy(gwT[:], ps[:, 0, C:C + E]).then_inc(wqT_ready, 1)
            act.wait_ge(ewT_mm, 2)
            for q in range(2):
                last = nc.scalar.copy(ewT[:, EH * q:EH * q + EH, :].rearrange("p e f -> p (e f)"), ps[:, 1 + q, :])
            last.then_inc(ewT_ready, 1)

            def ya(i, s):
                act.wait_ge(ya_mm, 2 * i + s + 1)
                earlier(act, za_mm[s], i)
                nc.scalar.copy(yT[s][0:Q], ps[0:Q, 0, 0:NS * Q]).then_inc(ya_ready, 1)

            def za(i, s):
                act.wait_ge(za_mm[s], i + 1)
                nc.scalar.mul(tt[s][0:Q, :, Q:2 * Q], ps[0:Q, 0, NS * Q:2 * NS * Q].rearrange("p (n c) -> p n c", n=NS), -1.0)
                nc.scalar.mul(da[s][Q:2 * Q, :, 0:Q], ps[Q:2 * Q, 0, 2 * NS * Q:3 * NS * Q].rearrange("p (n c) -> p n c", n=NS),
                              -1.0).then_inc(za_ready, 1)

            def y64_(i, s):
                act.wait_ge(y64_mm[s], i + 1)
                earlier(act, t12_mm[s], i)
                nc.scalar.copy(y64[s][:], ps[0:2 * Q, 2, 0:2 * NS * Q]).then_inc(y64_ready, 1)

            def wT_(i, s):
                act.wait_ge(wT_mm[s], i + 1)
                earlier(act, u_mm[NS - 1], 2 * i)
                nc.scalar.mul(wT[s][:], ps[:, 5, :], -1.0).then_inc(wT_ready, 1)

            def u_(i, s, n):
                act.wait_ge(u_mm[n], 2 * i + s + 1)
                earlier(act, sm_mm[n][1 - s], i + s)
                nc.scalar.copy(uu[:, n, 0:C], tiles(3 + n % 2)[:, n]).then_inc(u_ready[n], 1)

            def tt_(i, s):
                earlier(act, wT_mm[s], i)
                for b in range(NB):
                    r = slice(Q * b, Q * b + Q)
                    last = nc.scalar.copy(tt[s][r, :, Q * b:Q * b + Q],
                                          dT_all[r, :, bass.ds((2 * i + s) * NS, NS)].rearrange("p r n -> p n r"))
                last.then_inc(tt_set, 1)

            act.wait_ge(dT_done, 1)
            act.wait_ge(consts_ready, E + 4)
            def first2():
                tt_(0, 0)
                ya(0, 0)
                za(0, 0)
                y64_(0, 0)
                tt_(0, 1)
                ya(0, 1)
                wT_(0, 0)
                u_(0, 0, 0)

            def body2(i, s, ahead2, ahead1):
                nxt = after(i, s)
                u_(i, s, 1)
                if ahead1:
                    za(*nxt)
                u_(i, s, 2)
                if ahead1:
                    y64_(*nxt)
                if ahead2:
                    tt_(i + 1, s)
                u_(i, s, 3)
                if ahead2:
                    ya(i + 1, s)
                if ahead1:
                    wT_(*nxt)
                    u_(*nxt, 0)

            two_ahead(act, first2, body2)

            act.wait_ge(fold_mm, 1)
            nc.scalar.copy(mT[:], ps[:, 0, :]).then_inc(fold_out, 1)
            act.wait_ge(fold_mm, 2)
            nc.scalar.copy(mw[:], ps[:, 1, :]).then_inc(fold_out, 1)
            act.wait_ge(fold_mm, 3)
            nc.scalar.copy(gn[:].rearrange("p n c -> p (n c)"), ps[:, 2, :]).then_inc(fold_out, 1)

            def root(i, s, second):
                act.wait_ge(var_done, norms(i, s, second) + 1)
                nc.scalar.activation(sd[s][:, 0], ab[s][:, 0], ACT.Sqrt).then_inc(sd_done, 1)

            def tT_(i, s):
                act.wait_ge(tT_mm[s], i + 1)
                earlier(act, hid_mm[s], i)
                nc.scalar.activation(tT[s][:].rearrange("p n c -> p (n c)"), ps[:, 1, :], ACT.Identity, bias=mnb,
                                     scale=mng).then_inc(tT_ready, 1)

            def hid_(i, s):
                act.wait_ge(hid_mm[s], i + 1)
                earlier(act, out_mm[s], i)
                nc.scalar.activation(hid[s][:].rearrange("p n c -> p (n c)"), ps[:, 2, :], ACT.Relu,
                                     bias=b1c).then_inc(hid_ready, 1)

            def zT_(i, s):
                act.wait_ge(zT_mm[s], i + 1)
                nc.scalar.copy(zT[s][:].rearrange("p n c -> p (n c)"), ps[:, 1, :]).then_inc(zT_ready, 1)

            def zs_(i, s):
                earlier(act, zT_mm[s], i)
                act.wait_ge(nb_done, T + 2 * i + s + 1)
                for n in range(NS):
                    last = nc.scalar.activation(zv[s][:, n], x_all[:, 2 * i + s, n], ACT.Identity, bias=nb[s][:, n:n + 1],
                                                scale=rr[s][:, 0, n:n + 1])
                last.then_inc(z_ready, 1)

            def mask(i, s, n):
                b, k = n % 2, 4 * i + 2 * s + n // 2
                act.wait_ge(oh_ready, 2 * i + s + 1)
                act.wait_ge(ea_mm[b], k + 1)
                earlier(act, sum_done[b], k)
                for e in range(EH):
                    last = nc.scalar.activation(ea[b][:, e], ps[:, 4 + 2 * b, e * F:e * F + F], ACT.Copy,
                                                scale=oh[s][:, n, e:e + 1])
                last.then_inc(ea_done[b], 1)

            def first3():
                root(0, 0, 0)
                tT_(0, 0)
                hid_(0, 0)
                root(0, 0, 1)
                zs_(0, 0)
                root(0, 1, 0)
                zT_(0, 0)
                tT_(0, 1)
                hid_(0, 1)
                mask(0, 0, 0)
                root(0, 1, 1)
                mask(0, 0, 1)
                zs_(0, 1)
                mask(0, 0, 2)

            def body3(i, s, ahead2, ahead1):
                nxt = after(i, s)
                if ahead2:
                    root(i + 1, s, 0)
                if ahead1:
                    zT_(*nxt)
                if ahead2:
                    tT_(i + 1, s)
                mask(i, s, 3)
                if ahead2:
                    hid_(i + 1, s)
                if ahead1:
                    mask(*nxt, 0)
                if ahead2:
                    root(i + 1, s, 1)
                if ahead1:
                    mask(*nxt, 1)
                if ahead2:
                    zs_(i + 1, s)
                if ahead1:
                    mask(*nxt, 2)

            two_ahead(act, first3, body3)

        @block.vector
        def _(dve):
            bkvB = bkv[:, :]
            nc.vector.memset(sm[:], 0.0).then_inc(sm_ready[0], 1)

            def norm_a(s, k, src):
                for n in range(NS):
                    last = nc.vector.bn_stats(st[s][:, n], src(n))
                last.then_inc(stats_done, 1)
                dve.wait_ge(stats_done, k + 1)
                dve.sem_inc(dve_passed, 1)
                for n in range(NS):
                    last = nc.vector.bn_aggr(mv[s][:, n], st[s][:, n])
                last.then_inc(mv_done, 1)
                dve.wait_ge(mv_done, k + 1)
                nc.vector.tensor_scalar(ab[s][:, 0], mv[s][:, :, 1], EPS, None, ALU.add).then_inc(var_done, 1)

            def stats1(i, s):
                norm_a(s, 2 * i + s, lambda n: x_all[:, 2 * i + s, n])
                dve.wait_ge(var_done, 2 * i + s + 1)
                nc.vector.scalar_tensor_tensor(ab[s][:, 1], ab[s][:, 0], EPS, mv[s][:, :, 1], ALU.mult,
                                               ALU.add).then_inc(ab_done, 1)

            def scale1(i, s):
                dve.wait_ge(sd_done, 2 * i + s + 1)
                earlier(dve, h_done[s], i)
                nc.vector.reciprocal(rr[s][:], sd[s][:]).then_inc(rr_done, 1)
                dve.wait_ge(rr_done, 2 * i + s + 1)
                nc.vector.scalar_tensor_tensor(nb[s][:], mv[s][:, :, 0], -1.0, rr[s][:, 0], ALU.mult,
                                               ALU.mult).then_inc(nb_done, 1)
                earlier(dve, xT_mm[s], i)
                for n in range(NS):
                    last = nc.vector.tensor_scalar(xh[s][:, n], x_all[:, 2 * i + s, n], mv[s][:, n, 0:1],
                                                   rr[s][:, 1, n:n + 1], ALU.subtract, ALU.mult)
                last.then_inc(xh_ready, 1)

            def kv1(i, s):
                earlier(dve, kv_kept[s], 16 * i)
                earlier(dve, kT_mm[s], i)
                for n in range(NS):
                    dve.wait_ge(kv_mm[s], NS * i + n + 1)
                    nc.vector.tensor_tensor(kv[s][:, n], ps[:, 1 + n, 0:2 * C], bkvB, ALU.add).then_inc(kv_ready[s], 1)
                nc.vector.tensor_scalar(lr_all[:, bass.ds((2 * i + s) * NS, NS)], ps[:, 1:1 + NS, 2 * C], lrb[:, 0:1], None,
                                        ALU.add).then_inc(lr_ready, 1)

            def k1(i, s):
                dve.wait_ge(sn_done, 2 * i + s + 1)
                nc.vector.reciprocal(rn[s][:], sn[s][:]).then_inc(rn_done[s], 1)
                dve.wait_ge(rn_done[s], i + 1)
                dve.wait_ge(kv_ready[s], NS * (i + 1))
                for n in range(NS):
                    last = nc.vector.tensor_scalar(kv[s][:, n, 0:C], kv[s][:, n, 0:C], rn[s][:, n:n + 1], None, ALU.mult)
                last.then_inc(k_ready, 1)

            def first1():
                dve.wait_ge(x_loaded[0], 16)
                stats1(0, 0)
                scale1(0, 0)
                dve.wait_ge(x_loaded[1], 16)
                stats1(0, 1)
                scale1(0, 1)
                dve.wait_ge(x_rest, 16 * (T - 2))
                dve.wait_ge(kvw_loaded, 16 * 6)

            def body1(i, s, ahead2, ahead1):
                nxt = after(i, s)
                kv1(i, s)
                if ahead2:
                    stats1(i + 1, s)
                k1(i, s)
                if ahead2:
                    scale1(i + 1, s)

            two_ahead(dve, first1, body1)

            dve.wait_ge(w_loaded, 16 * 10)
            nc.vector.tensor_copy(bqB[:], bqc.broadcast_to([P, P])).then_inc(bqB_ready, 1)

            for s in range(2):
                dve.wait_ge(gd_done[s], NB * NIT)
            nc.vector.transpose(lt[:].rearrange("p c r -> p (c r)"), gd_all[:].rearrange("p c t -> p (c t)")).then_inc(lt_done, 1)
            dve.wait_ge(lt_done, 1)
            dve.wait_ge(xi_ready, 1)
            for j in range(Q - 1):
                m, w = Q - 1 - j, j + 1
                below = prod[:, 0:m * w].rearrange("p (i k) -> p i k", k=w)
                if j:
                    dve.wait_ge(elim, 2 * j)
                nc.vector.tensor_tensor(below, lt[:, j, j + 1:Q].unsqueeze(2).broadcast_to([P, m, w]),
                                        xi[:, j, 0:w].unsqueeze(1).broadcast_to([P, m, w]), ALU.mult).then_inc(elim, 1)
                dve.wait_ge(elim, 2 * j + 1)
                nc.vector.tensor_tensor(xi[:, j + 1:Q, 0:w], xi[:, j + 1:Q, 0:w], below, ALU.subtract).then_inc(elim, 1)
            dve.wait_ge(elim, 2 * (Q - 1))
            nc.vector.transpose(dT_all[:].rearrange("p r t -> p (r t)"), xi[:].rearrange("p r c -> p (r c)")).then_inc(dT_done, 1)
            nc.vector.transpose(d_all[:], xi[:].rearrange("p r c -> p c r")).then_inc(d_done, 1)

            def yb(i, s):
                dve.wait_ge(yb_mm, 2 * i + s + 1)
                earlier(dve, zb_mm[s], i)
                nc.vector.tensor_copy(yT[s][2 * Q:3 * Q].rearrange("p n c -> p (n c)"),
                                      ps[2 * Q:3 * Q, 1, 0:NS * Q]).then_inc(yb_ready, 1)

            def zb(i, s):
                dve.wait_ge(zb_mm[s], i + 1)
                nc.vector.tensor_scalar(tt[s][2 * Q:3 * Q, :, 3 * Q:4 * Q],
                                        ps[2 * Q:3 * Q, 1, NS * Q:2 * NS * Q].rearrange("p (n c) -> p n c", n=NS), -1.0, None,
                                        ALU.mult).then_inc(zb_ready, 1)

            def t12(i, s):
                dve.wait_ge(t12_mm[s], i + 1)
                nc.vector.tensor_scalar(tt[s][0:2 * Q, :, 2 * Q:4 * Q],
                                        ps[0:2 * Q, 2, 2 * NS * Q:4 * NS * Q].rearrange("p (n c) -> p n c", n=NS), -1.0, None,
                                        ALU.mult).then_inc(t12_ready, 1)

            def lru(i, s, n):
                dve.wait_ge(u_ready[n], 2 * i + s + 1)
                nc.vector.tensor_scalar(uu[:, n, C:2 * C], uu[:, n, 0:C], lr_all[:, bass.ds((2 * i + s) * NS + n, 1)], None,
                                        ALU.mult).then_inc(lru_ready[n], 1)

            def add_sm(i, s, n):
                dve.wait_ge(sm_mm[n][s], i + 1)
                nc.vector.tensor_tensor(sm[:, n], ps[:, 6 + n % 2, 0:2 * C], sm[:, n], ALU.add).then_inc(sm_ready[n], 1)

            def da_(i, s):
                earlier(dve, t12_mm[s], i)
                at = bass.ds((2 * i + s) * NS, NS)
                for b in range(NB - 1):
                    r = slice(Q * b, Q * b + Q)
                    last = nc.vector.tensor_copy(da[s][r, :, Q * (b % 2):Q * (b % 2) + Q], d_all[r, :, at].rearrange("p r n -> p n r"))
                last.then_inc(da_set, 1)

            dve.wait_ge(d_done, 1)
            dve.wait_ge(consts_ready, E + 4)
            def first2():
                da_(0, 0)
                yb(0, 0)
                zb(0, 0)
                t12(0, 0)
                da_(0, 1)
                yb(0, 1)
                zb(0, 1)

            def body2(i, s, ahead2, ahead1):
                nxt = after(i, s)
                lru(i, s, 0)
                lru(i, s, 1)
                lru(i, s, 2)
                add_sm(i, s, 0)
                if ahead1:
                    t12(*nxt)
                lru(i, s, 3)
                add_sm(i, s, 1)
                if ahead2:
                    da_(i + 1, s)
                    yb(i + 1, s)
                add_sm(i, s, 2)
                if ahead2:
                    zb(i + 1, s)
                add_sm(i, s, 3)

            two_ahead(dve, first2, body2)

            dve.wait_ge(fold_mm, 4)
            nc.vector.tensor_tensor(cb[:], tiles(3), bo[:, :].unsqueeze(1).broadcast_to([P, NS, C]), ALU.add).then_inc(cb_ready, 1)

            def inverse_root(s, k):
                dve.wait_ge(sd_done, k + 1)
                nc.vector.reciprocal(rr[s][:, 0], sd[s][:, 0]).then_inc(rr_done, 1)
                dve.wait_ge(rr_done, k + 1)

            def resid(i, s):
                dve.wait_ge(dl_mm[s], i + 1)
                dve.wait_ge(hcb_ready, 2 * i + s + 1)
                nc.vector.tensor_tensor(h_all[:, 2 * i + s], tiles(0), h_all[:, 2 * i + s], ALU.add).then_inc(h2_ready[s], 1)
                dve.wait_ge(h2_ready[s], i + 1)
                dve.sem_inc(dve_passed, 1)
                norm_a(s, norms(i, s, 0), lambda n: h_all[:, 2 * i + s, n])

            def tn_(i, s):
                inverse_root(s, norms(i, s, 0))
                earlier(dve, tT_mm[s], i)
                for n in range(NS):
                    last = nc.vector.tensor_scalar(tnv[s][:, n], h_all[:, 2 * i + s, n], mv[s][:, n, 0:1], rr[s][:, 0, n:n + 1],
                                                   ALU.subtract, ALU.mult)
                last.then_inc(tn_ready, 1)

            def mlp_out(i, s):
                dve.wait_ge(out_mm[s], i + 1)
                dve.wait_ge(xb_ready[s], i + 1)
                nc.vector.tensor_tensor(x_all[:, 2 * i + s], tiles(2), x_all[:, 2 * i + s], ALU.add).then_inc(x1_ready[s], 1)
                dve.wait_ge(x1_ready[s], i + 1)
                dve.sem_inc(dve_passed, 1)
                norm_a(s, norms(i, s, 1), lambda n: x_all[:, 2 * i + s, n])

            def zscale(i, s):
                inverse_root(s, norms(i, s, 1))
                nc.vector.scalar_tensor_tensor(nb[s][:], mv[s][:, :, 0], -1.0, rr[s][:, 0], ALU.mult,
                                               ALU.mult).then_inc(nb_done, 1)

            def choose(i, s):
                def link(ins, k):
                    ins.then_inc(oh_step[s], 1)
                    dve.wait_ge(oh_step[s], 4 * i + k)
                scores = ps[:, 3, 0:NS * E].rearrange("p (n e) -> p n e", n=NS)
                dve.wait_ge(gate_mm, 2 * i + s + 1)
                link(nc.vector.tensor_reduce(mx[s][:], scores, AX_X, ALU.max), 1)
                link(nc.vector.tensor_tensor(eq[s][:], scores, mx[s][:].unsqueeze(2).broadcast_to([P, NS, E]), ALU.is_equal), 2)
                link(nc.vector.tensor_tensor(eq[s][:], eq[s][:], desc[:, :].unsqueeze(1).broadcast_to([P, NS, E]), ALU.mult), 3)
                link(nc.vector.tensor_reduce(m2[s][:], eq[s][:], AX_X, ALU.max), 4)
                nc.vector.tensor_tensor(oh[s][:], eq[s][:], m2[s][:].unsqueeze(2).broadcast_to([P, NS, E]),
                                        ALU.is_equal).then_inc(oh_ready, 1)

            def mask(i, s, n):
                b, k = n % 2, 4 * i + 2 * s + n // 2
                dve.wait_ge(oh_ready, 2 * i + s + 1)
                dve.wait_ge(ed_mm[b], k + 1)
                earlier(dve, sum_done[b], k)
                nc.vector.tensor_tensor(ed[b], ps[:, 5 + 2 * b, :].rearrange("p (e f) -> p e f", e=EH),
                                        oh[s][:, n, EH:E].unsqueeze(2).broadcast_to([P, EH, F]), ALU.mult).then_inc(ed_done[b], 1)

            def join(i, s, n):
                b, k = n % 2, 4 * i + 2 * s + n // 2
                dve.wait_ge(ed_done[b], k + 1)
                dve.wait_ge(ea_done[b], k + 1)
                earlier(dve, add_step[b], ADDS * k)
                nc.vector.tensor_tensor(es[b], ed[b], ea[b], ALU.add).then_inc(sum_done[b], 1)

            def first3():
                resid(0, 0)
                tn_(0, 0)
                mlp_out(0, 0)
                zscale(0, 0)
                resid(0, 1)
                tn_(0, 1)
                choose(0, 0)
                mlp_out(0, 1)
                mask(0, 0, 0)
                zscale(0, 1)
                join(0, 0, 0)

            def body3(i, s, ahead2, ahead1):
                nxt = after(i, s)
                if ahead2:
                    resid(i + 1, s)
                mask(i, s, 1)
                if ahead2:
                    tn_(i + 1, s)
                join(i, s, 1)
                mask(i, s, 2)
                join(i, s, 2)
                mask(i, s, 3)
                join(i, s, 3)
                if ahead1:
                    choose(*nxt)
                if ahead2:
                    mlp_out(i + 1, s)
                if ahead1:
                    mask(*nxt, 0)
                if ahead2:
                    zscale(i + 1, s)
                if ahead1:
                    join(*nxt, 0)

            dve.wait_ge(consts_ready, E + 4)
            two_ahead(dve, first3, body3)

        @block.tensor
        def _(pe):
            pe.wait_ge(id_ready, 1)
            pe.wait_ge(kvw_loaded, 16 * 6)

            def four(bank, lhsT, rhs, ready, step=1):
                for n in range(NS):
                    last = nc.tensor.matmul(tiles(bank)[:, n], lhsT(n), rhs(n), start=True, stop=True)
                last.then_inc(ready, step)

            def turn(bank, src, ready):
                for n in range(NS):
                    last = nc.tensor.transpose(tiles(bank)[:, n], src(n), ident[:])
                last.then_inc(ready, 1)

            def xT1(i, s):
                pe.wait_ge(xh_ready, 2 * i + s + 1)
                earlier(pe, xnT_ready, 2 * i + s)
                turn(0, lambda n: xh[s][:, n], xT_mm[s])

            def kvm1(i, s):
                pe.wait_ge(xnT_ready, 2 * i + s + 1)
                earlier(pe, lr_ready, 2 * i + s)
                for n in range(NS):
                    nc.tensor.matmul(ps[:, 1 + n, 0:KVW], xnT[s][:, n * P:n * P + P], wkvl[:], start=True,
                                     stop=True).then_inc(kv_mm[s], 1)

            def kT1(i, s):
                pe.wait_ge(k_ready, 2 * i + s + 1)
                earlier(pe, kT_ready, 2 * i + s)
                turn(5, lambda n: kv[s][:, n, 0:C], kT_mm[s])

            def gram1(i, s):
                pe.wait_ge(kT_ready, 2 * i + s + 1)
                earlier(pe, g_ready, 2 * i + s)
                four(6, lambda n: kT[s][:, n * P:n * P + P], lambda n: kT[s][:, n * P:n * P + P], g_mm[s])

            def first1():
                xT1(0, 0)
                kvm1(0, 0)
                xT1(0, 1)

            def body1(i, s, ahead2, ahead1):
                nxt = after(i, s)
                if ahead1:
                    kvm1(*nxt)
                kT1(i, s)
                if ahead2:
                    xT1(i + 1, s)
                gram1(i, s)

            two_ahead(pe, first1, body1)

            pe.wait_ge(xnT_ready, T)
            pe.wait_ge(lr_ready, T)
            pe.wait_ge(e_loaded, 32)
            pe.wait_ge(w_loaded, 16 * 10)
            nc.tensor.transpose(ps[:, 0, 0:C], wq[:], ident[:])
            nc.tensor.transpose(ps[:, 0, C:C + E], gw[:], ident[0:E, 0:E]).then_inc(wqT_mm, 1)
            for q in range(2):
                turn(1 + q, lambda n: ew[:, EH * q + n], ewT_mm)

            pe.wait_ge(wqT_ready, 1)
            pe.wait_ge(ewT_ready, 1)
            pe.wait_ge(kT_ready, T)
            pe.wait_ge(g_ready, T)

            def ya(i, s):
                pe.wait_ge(tt_set, 2 * i + s + 1)
                pe.wait_ge(gs_loaded[s], 16 * (i + 1))
                earlier(pe, za_ready, 2 * i + s)
                earlier(pe, zb_ready, 2 * i + s)
                pe.sem_inc(pe_passed, 1)
                for bank, lo, ready in ((0, 0, ya_mm), (1, 2 * Q, yb_mm)):
                    hi = lo + Q
                    for n in range(NS):
                        last = nc.tensor.matmul(ps[lo:lo + Q, bank, n * Q:n * Q + Q], gs[s][hi:hi + Q, n, lo:lo + Q],
                                                tt[s][hi:hi + Q, n, hi:hi + Q], start=True, stop=True)
                    last.then_inc(ready, 1)

            def za(i, s):
                pe.wait_ge(ya_ready, 2 * i + s + 1)
                pe.wait_ge(da_set, 2 * i + s + 1)
                pe.sem_inc(pe_passed, 1)
                for n in range(NS):
                    nc.tensor.matmul(ps[0:Q, 0, (NS + n) * Q:(NS + n + 1) * Q], da[s][0:Q, n, 0:Q], yT[s][0:Q, n],
                                     start=True, stop=True)
                for n in range(NS):
                    last = nc.tensor.matmul(ps[Q:2 * Q, 0, (2 * NS + n) * Q:(2 * NS + n + 1) * Q], yT[s][0:Q, n],
                                            da[s][0:Q, n, 0:Q], start=True, stop=True)
                last.then_inc(za_mm[s], 1)
                pe.wait_ge(yb_ready, 2 * i + s + 1)
                pe.sem_inc(pe_passed, 1)
                for n in range(NS):
                    last = nc.tensor.matmul(ps[2 * Q:3 * Q, 1, (NS + n) * Q:(NS + n + 1) * Q], da[s][2 * Q:3 * Q, n, 0:Q],
                                            yT[s][2 * Q:3 * Q, n], start=True, stop=True)
                last.then_inc(zb_mm[s], 1)

            def y64_(i, s):
                pe.wait_ge(zb_ready, 2 * i + s + 1)
                earlier(pe, t12_ready, 2 * i + s)
                pe.sem_inc(pe_passed, 1)
                for n in range(NS):
                    last = nc.tensor.matmul(ps[0:2 * Q, 2, 2 * n * Q:2 * (n + 1) * Q], gs[s][2 * Q:4 * Q, n, 0:2 * Q],
                                            tt[s][2 * Q:4 * Q, n, 2 * Q:4 * Q], start=True, stop=True)
                last.then_inc(y64_mm[s], 1)

            def t12(i, s):
                pe.wait_ge(y64_ready, 2 * i + s + 1)
                pe.wait_ge(za_ready, 2 * i + s + 1)
                pe.sem_inc(pe_passed, 1)
                for n in range(NS):
                    last = nc.tensor.matmul(ps[0:2 * Q, 2, 2 * (NS + n) * Q:2 * (NS + n + 1) * Q], da[s][0:2 * Q, n, :],
                                            y64[s][:, n], start=True, stop=True)
                last.then_inc(t12_mm[s], 1)

            def uv(i, s):
                pe.wait_ge(t12_ready, 2 * i + s + 1)
                pe.wait_ge(kvs_loaded[s], 16 * (i + 1))
                earlier(pe, u_ready[2], 2 * i + s)
                earlier(pe, u_ready[3], 2 * i + s)
                for n in range(NS):
                    nc.tensor.matmul(tiles(3 + n % 2)[:, n], tt[s][:, n], kvs[s][:, n, C:2 * C], start=n < 2, stop=False,
                                     skip_group_check=True)

            def wT_(i, s):
                pe.wait_ge(t12_ready, 2 * i + s + 1)
                pe.wait_ge(kvs_loaded[s], 16 * (i + 1))
                earlier(pe, wT_ready, 2 * i + s)
                four(5, lambda n: kvs[s][:, n, 0:C], lambda n: tt[s][:, n], wT_mm[s])

            def u_(i, s, n):
                if n == 0:
                    pe.wait_ge(wT_ready, 2 * i + s + 1)
                if n >= 2:
                    pe.wait_ge(u_ready[n - 2], 2 * i + s + 1)
                earlier(pe, sm_ready[n], 2 * i + s + (1 if n == 0 else 0))
                nc.tensor.matmul(tiles(3 + n % 2)[:, n], wT[s][:, n], sm[:, n, 0:C], start=False, stop=True,
                                 skip_group_check=True).then_inc(u_mm[n], 1)

            def sm_(i, s, n):
                pe.wait_ge(lru_ready[n], 2 * i + s + 1)
                if n >= 2:
                    pe.wait_ge(sm_ready[n - 2], 2 * i + s + (2 if n == 2 else 1))
                nc.tensor.matmul(ps[:, 6 + n % 2, 0:2 * C], kvs[s][:, n, 0:C], uu[:, n], start=True,
                                 stop=True).then_inc(sm_mm[n][s], 1)

            def first2():
                ya(0, 0)
                za(0, 0)
                y64_(0, 0)
                t12(0, 0)
                ya(0, 1)
                uv(0, 0)
                wT_(0, 0)
                za(0, 1)
                pe.wait_ge(sm_ready[0], 1)
                u_(0, 0, 0)
                u_(0, 0, 1)
                y64_(0, 1)
                u_(0, 0, 2)
                u_(0, 0, 3)
                sm_(0, 0, 0)

            def body2(i, s, ahead2, ahead1):
                nxt = after(i, s)
                sm_(i, s, 1)
                if ahead1:
                    t12(*nxt)
                sm_(i, s, 2)
                if ahead2:
                    ya(i + 1, s)
                if ahead1:
                    uv(*nxt)
                    wT_(*nxt)
                if ahead2:
                    za(i + 1, s)
                sm_(i, s, 3)
                if ahead1:
                    u_(*nxt, 0)
                    u_(*nxt, 1)
                if ahead2:
                    y64_(i + 1, s)
                if ahead1:
                    u_(*nxt, 2)
                    u_(*nxt, 3)
                    sm_(*nxt, 0)

            two_ahead(pe, first2, body2)

            for n in range(NS):
                pe.wait_ge(sm_ready[n], T + (1 if n == 0 else 0))
            turn(0, lambda n: sm[:, n, C:2 * C], fold_mm)
            pe.wait_ge(fold_out, 1)
            four(1, lambda n: mT[:, n * C:n * C + C], lambda n: wo[:], fold_mm)
            pe.wait_ge(fold_out, 2)
            nc.tensor.matmul(ps[:, 2, :], wqT[:], mw[:], start=True, stop=True).then_inc(fold_mm, 1)
            pe.wait_ge(bqB_ready, 1)
            nc.tensor.matmul(ps[:, 3, :], bqB[:], mw[:], start=True, stop=True).then_inc(fold_mm, 1)
            pe.wait_ge(fold_out, 3)
            pe.wait_ge(cb_ready, 1)

            def delta(i, s):
                pe.wait_ge(xns_loaded[s], 16 * (i + 1))
                earlier(pe, h2_ready[1 - s], i + s)
                four(0, lambda n: xns[s][:, n], lambda n: gn[:, n], dl_mm[s])

            def tT_(i, s):
                pe.wait_ge(tn_ready, 2 * i + s + 1)
                earlier(pe, zT_ready, 2 * i + s)
                turn(1, lambda n: tnv[s][:, n], tT_mm[s])

            def hid_(i, s):
                pe.wait_ge(tT_ready, 2 * i + s + 1)
                earlier(pe, x1_ready[1 - s], i + s)
                nc.tensor.matmul(ps[:, 2, :], w1s[:], tT[s][:].rearrange("p n c -> p (n c)"), start=True,
                                 stop=True).then_inc(hid_mm[s], 1)

            def out_(i, s):
                pe.wait_ge(hid_ready, 2 * i + s + 1)
                four(2, lambda n: hid[s][:, n], lambda n: w2s[:], out_mm[s])

            def zT_(i, s):
                pe.wait_ge(z_ready, 2 * i + s + 1)
                pe.wait_ge(tT_ready, 2 * i + s + 1)
                turn(1, lambda n: zv[s][:, n], zT_mm[s])

            def gate(i, s):
                pe.wait_ge(zT_ready, 2 * i + s + 1)
                earlier(pe, oh_ready, 2 * i + s)
                for n in range(NS):
                    last = nc.tensor.matmul(ps[:, 3, n * E:n * E + E], zT[s][:, n], gwT[:], start=True, stop=True)
                last.then_inc(gate_mm, 1)

            def experts(i, s, n):
                b, k = n % 2, 4 * i + 2 * s + n // 2
                for half, bank, used, ready in ((0, 4 + 2 * b, ea_done, ea_mm), (1, 5 + 2 * b, ed_done, ed_mm)):
                    earlier(pe, used[b], k)
                    nc.tensor.matmul(ps[:, bank, :], zT[s][:, n],
                                     ewT[:, EH * half:EH * half + EH, :].rearrange("p e f -> p (e f)"), start=True,
                                     stop=True).then_inc(ready[b], 1)

            def first3():
                delta(0, 0)
                tT_(0, 0)
                hid_(0, 0)
                delta(0, 1)
                out_(0, 0)
                zT_(0, 0)

            def body3(i, s, ahead2, ahead1):
                nxt = after(i, s)
                if ahead1:
                    tT_(*nxt)
                gate(i, s)
                if ahead1:
                    hid_(*nxt)
                if ahead2:
                    delta(i + 1, s)
                if ahead1:
                    out_(*nxt)
                experts(i, s, 0)
                experts(i, s, 1)
                experts(i, s, 2)
                if ahead1:
                    zT_(*nxt)
                experts(i, s, 3)

            pe.wait_ge(ewI_ready, 1)
            two_ahead(pe, first3, body3)


_INS = ["x", "dn_g", "dn_b", "gates_w", "gates_b", "lr_w", "lr_b", "out_w", "out_b", "mn_g", "mn_b", "w1", "b1", "w2", "b2"]


def kernel(**inputs):
    import numpy as _np
    import concourse.bacc as _bacc
    from concourse import mybir as _mybir
    from concourse.bass_utils import run_bass_kernel_spmd as _run

    nc = _bacc.Bacc("TRN2", target_bir_lowering=False, num_devices=1)
    arrays, args = {}, []
    for name in [f"L0_attn_{n}" for n in _INS] + ["L0_ffn_gate_w", "L0_ffn_expert_w"]:
        a = _np.ascontiguousarray(inputs[name])
        arrays[f"in_{name}_dram"] = a
        args.append(nc.dram_tensor(f"in_{name}_dram", a.shape, _mybir.dt.from_np(a.dtype), kind="ExternalInput").ap())
    shape = inputs["L0_attn_x"].shape
    args.append(nc.dram_tensor("out_dram", shape, _mybir.dt.float32, kind="ExternalOutput").ap())
    delta_block_kernel(nc, *args)
    r = _run(nc, [arrays], core_ids=[0])
    return r.results[0]["out_dram"]
```

```python
from contextlib import ExitStack

import concourse.bass as bass
from concourse import mybir

P = 128
Q = 32
EPS = 1e-5

ALU = mybir.AluOpType
ACT = mybir.ActivationFunctionType
AX_X = mybir.AxisListType.X
F32 = mybir.dt.float32


def delta_block_kernel(
    nc: bass.Bass,
    x: bass.AP, dn_g: bass.AP, dn_b: bass.AP, gates_w: bass.AP, gates_b: bass.AP,
    lr_w: bass.AP, lr_b: bass.AP, out_w: bass.AP, out_b: bass.AP,
    mn_g: bass.AP, mn_b: bass.AP, w1: bass.AP, b1: bass.AP, w2: bass.AP, b2: bass.AP,
    gate_w: bass.AP, expert_w: bass.AP,
    out: bass.AP,
):
    NS, L, C = x.shape
    E, F, _ = expert_w.shape
    T = L // P
    NIT = T // 2
    NB = P // Q
    TN = T * NS
    KVW = 2 * C + 1
    EH = E // 2
    ADDS = 3
    assert C == P and F == P and NS == 4 and TN == Q and E == 8 and T % 2 == 0

    x_v = x.rearrange("n (t p) c -> p t n c", p=P)
    out_v = out.rearrange("n (t p) c -> p t n c", p=P)

    with ExitStack() as ctx:
        def sb(name, shape):
            return ctx.enter_context(nc.sbuf_tensor(name, shape, F32))

        def sem(name):
            return ctx.enter_context(nc.semaphore(name))

        def pair(name):
            return [sem(f"{name}{s}") for s in range(2)]

        def each(name):
            return [sem(f"{name}{n}") for n in range(NS)]

        ps = ctx.enter_context(nc.psum_tensor("ps", [P, 8, 512], F32))

        def tiles(bank, width=P):
            return ps[:, bank, 0:NS * width].rearrange("p (n c) -> p n c", n=NS)

        ident = sb("ident", [P, P])
        desc = sb("desc", [P, E])
        epsc = sb("epsc", [P, 1])
        wq = sb("wq", [P, C])
        wqT = sb("wqT", [P, C])
        wkvl = sb("wkvl", [P, KVW])
        bkv = sb("bkv", [P, 2 * C])
        lrb = sb("lrb", [P, 1])
        wo = sb("wo", [P, C])
        bo = sb("bo", [P, C])
        w1s = sb("w1s", [P, C])
        w2s = sb("w2s", [P, C])
        b2s = sb("b2s", [P, C])
        cols = sb("cols", [P, 6])
        dng, dnb, mng, mnb, b1c, bqc = [cols[:, j:j + 1] for j in range(6)]
        bqB = sb("bqB", [P, P])
        gw = sb("gw", [E, C])
        gwT = sb("gwT", [P, E])
        ew = sb("ew", [P, E, C])
        ewT = sb("ewT", [P, E, F])

        x_all = sb("x_all", [P, T, NS, C])
        h_all = sb("h_all", [P, T, NS, C])
        xnT_all = sb("xnT_all", [P, T, NS * P])
        kv_all = sb("kv_all", [P, T, NS * 2 * C])
        g_all = sb("g_all", [P, T, NS * P])
        lr_all = sb("lr_all", [P, TN])
        gd_all = sb("gd_all", [P, Q, TN])
        lt = sb("lt", [P, Q, Q])
        xi = sb("xi", [P, Q, Q])
        prod = sb("prod", [P, Q * Q])
        dT_all = sb("dT_all", [P, Q, TN])
        d_all = sb("d_all", [P, Q, TN])

        st = [sb(f"st{s}", [P, NS, 6]) for s in range(2)]
        mv = [sb(f"mv{s}", [P, NS, 2]) for s in range(2)]
        ab = [sb(f"ab{s}", [P, 2, NS]) for s in range(2)]
        sd = [sb(f"sd{s}", [P, 2, NS]) for s in range(2)]
        rr = [sb(f"rr{s}", [P, 2, NS]) for s in range(2)]
        nb = [sb(f"nb{s}", [P, NS]) for s in range(2)]
        nb0 = [sb(f"nb0{s}", [P, 2]) for s in range(2)]
        xh = [sb(f"xh{s}", [P, NS, C]) for s in range(2)]
        xnT = [sb(f"xnT{s}", [P, NS * P]) for s in range(2)]
        kv = [sb(f"kv{s}", [P, NS, 2 * C]) for s in range(2)]
        sq = sb("sq", [P, NS, C])
        ss = [sb(f"ss{s}", [P, NS]) for s in range(2)]
        sn = [sb(f"sn{s}", [P, NS]) for s in range(2)]
        rn = [sb(f"rn{s}", [P, NS]) for s in range(2)]
        kT = [sb(f"kT{s}", [P, NS * P]) for s in range(2)]
        gg = [sb(f"gg{s}", [P, NS, P]) for s in range(2)]

        kvs = [sb(f"kvs{s}", [P, NS, 2 * C]) for s in range(2)]
        gs = [sb(f"gs{s}", [P, NS, P]) for s in range(2)]
        tt = [sb(f"tt{s}", [P, NS, P]) for s in range(2)]
        da = [sb(f"da{s}", [P, NS, 2 * Q]) for s in range(2)]
        yT = [sb(f"yT{s}", [P, NS, Q]) for s in range(2)]
        y64 = [sb(f"y64{s}", [2 * Q, NS, 2 * Q]) for s in range(2)]
        wT = [sb(f"wT{s}", [P, NS, P]) for s in range(2)]
        uu = sb("uu", [P, NS, 2 * C])
        sm = sb("sm", [P, NS, 2 * C])

        mT = sb("mT", [P, NS * C])
        mw = sb("mw", [P, NS * C])
        gn = sb("gn", [P, NS, C])
        cb = sb("cb", [P, NS, C])

        xns = [sb(f"xns{s}", [P, NS, P]) for s in range(2)]
        tn, z = xnT, kT
        tnv = [t[:, :].rearrange("p (n c) -> p n c", n=NS) for t in tn]
        zv = [t[:, :].rearrange("p (n c) -> p n c", n=NS) for t in z]
        tT = gg
        hid = wT
        zT = tt
        mx = [sb(f"mx{s}", [P, NS]) for s in range(2)]
        eq = [sb(f"eq{s}", [P, NS, E]) for s in range(2)]
        m2 = [sb(f"m2{s}", [P, NS]) for s in range(2)]
        oh = [sb(f"oh{s}", [P, NS, E]) for s in range(2)]
        ea, ed, es = [[t[:, :, :].rearrange("p a b -> p (a b)")[:, b * EH * F:(b + 1) * EH * F].rearrange("p (e f) -> p e f", e=EH)
                       for b in range(2)] for t in (gd_all, lt, xi)]

        x_loaded, x_rest, e_loaded = pair("x_loaded"), sem("x_rest"), sem("e_loaded")
        kvw_loaded, w_loaded = sem("kvw_loaded"), sem("w_loaded")
        id_zero, id_ready, consts_ready = sem("id_zero"), sem("id_ready"), sem("consts_ready")
        bqB_ready, wqT_mm, wqT_ready = sem("bqB_ready"), sem("wqT_mm"), sem("wqT_ready")
        stats_done, mv_done, ab_done = sem("stats_done"), sem("mv_done"), sem("ab_done")
        sd_done, rr_done, nb_done, h_done = sem("sd_done"), sem("rr_done"), sem("nb_done"), pair("h_done")
        xh_ready, xT_mm, xnT_ready, xnT_kept = sem("xh_ready"), pair("xT_mm"), sem("xnT_ready"), pair("xnT_kept")
        kv_mm, kv_ready, lr_ready = pair("kv_mm"), pair("kv_ready"), sem("lr_ready")
        ss_done, sn_done, rn_done, k_ready, kv_kept = (sem("ss_done"), sem("sn_done"), pair("rn_done"),
                                                       sem("k_ready"), pair("kv_kept"))
        kT_mm, kT_ready, g_mm, g_ready, g_kept, gd_done = (pair("kT_mm"), sem("kT_ready"), pair("g_mm"),
                                                           sem("g_ready"), pair("g_kept"), pair("gd_done"))
        last_gd_done = sem("last_gd_done")
        xi_ready, lt_done, elim, dT_done, d_done = (sem("xi_ready"), sem("lt_done"), sem("elim"), sem("dT_done"),
                                                    sem("d_done"))
        ewT_mm, ewT_ready, gwT_ready = sem("ewT_mm"), sem("ewT_ready"), sem("gwT_ready")
        kvs_loaded, gs_loaded = pair("kvs_loaded"), pair("gs_loaded")
        tt_set, da_set = sem("tt_set"), sem("da_set")
        ya_mm, yb_mm, ya_ready, yb_ready = sem("ya_mm"), sem("yb_mm"), sem("ya_ready"), sem("yb_ready")
        za_mm, zb_mm, za_ready, zb_ready = pair("za_mm"), pair("zb_mm"), sem("za_ready"), sem("zb_ready")
        y64_mm, y64_ready, t12_mm, t12_ready = pair("y64_mm"), sem("y64_ready"), pair("t12_mm"), sem("t12_ready")
        wT_mm, wT_ready = pair("wT_mm"), sem("wT_ready")
        u_mm, u_ready, lru_ready, sm_ready = each("u_mm"), each("u_ready"), each("lru_ready"), each("sm_ready")
        sm_mm = [pair(f"sm_mm{n}_") for n in range(NS)]
        fold_mm, fold_out, cb_ready = sem("fold_mm"), sem("fold_out"), sem("cb_ready")
        xns_loaded, dl_mm, hcb_ready, h2_ready = pair("xns_loaded"), pair("dl_mm"), sem("hcb_ready"), pair("h2_ready")
        tn_ready, tT_mm, tT_ready, xb_ready = sem("tn_ready"), pair("tT_mm"), sem("tT_ready"), pair("xb_ready")
        hid_mm, hid_ready, out_mm, x1_ready = pair("hid_mm"), sem("hid_ready"), pair("out_mm"), pair("x1_ready")
        z_ready, zT_mm, zT_ready, ewI_ready = sem("z_ready"), pair("zT_mm"), sem("zT_ready"), sem("ewI_ready")
        gate_mm, oh_step, oh_ready = sem("gate_mm"), pair("oh_step"), sem("oh_ready")
        ea_mm, ed_mm, ea_done, ed_done, sum_done = (pair("ea_mm"), pair("ed_mm"), pair("ea_done"), pair("ed_done"),
                                                     pair("sum_done"))
        nb0_done, tnb_ready = sem("nb0_done"), sem("tnb_ready")
        add_step, stored = pair("add_step"), sem("stored")

        dve_passed, pe_passed = sem("dve_passed"), sem("pe_passed")

        block = ctx.enter_context(nc.Block())

        def earlier(eng, semaphore, value):
            if not isinstance(value, int) or value > 0:
                eng.wait_ge(semaphore, value)

        def norms(i, s, second):
            return T + 2 * (2 * i + s) + second

        def after(i, s):
            return (i, 1) if s == 0 else (i + 1, 0)

        def two_ahead(eng, first, body):
            first()
            body(0, 0, True, True)
            body(0, 1, True, True)
            with eng.Fori(1, NIT - 1) as i:
                body(i, 0, True, True)
                body(i, 1, True, True)
            body(NIT - 1, 0, False, True)
            body(NIT - 1, 1, False, False)

        def in_turn(eng, body):
            body(0, 0)
            body(0, 1)
            with eng.Fori(1, NIT) as i:
                body(i, 0)
                body(i, 1)

        def total(eng, add, i, s, n):
            b, k = n % 2, 4 * i + 2 * s + n // 2
            eng.wait_ge(sum_done[b], k + 1)
            add(es[b][:, 0:2], es[b][:, 0:2], es[b][:, 2:4], ALU.add).then_inc(add_step[b], 1)
            eng.wait_ge(add_step[b], ADDS * k + 1)
            add(es[b][:, 0], es[b][:, 0], es[b][:, 1], ALU.add).then_inc(add_step[b], 1)
            eng.wait_ge(add_step[b], ADDS * k + 2)
            add(x_all[:, 2 * i + s, n], es[b][:, 0], x_all[:, 2 * i + s, n], ALU.add).then_inc(add_step[b], 1)

        def last_diagonals(copy, first):
            for b in range(first, first + 2):
                r = slice(Q * b, Q * b + Q)
                copy(gd_all[r, :, (T - 1) * NS:T * NS].rearrange("p c n -> p n c"),
                     tiles(6)[r, :, Q * b:Q * b + Q]).then_inc(last_gd_done, 1)

        @block.sync
        def _(sp):
            sp.dma_start(x_all[:, 0], x_v[:, 0]).then_inc(x_loaded[0], 16)
            for dst, src in ((dng, dn_g.unsqueeze(1)), (dnb, dn_b.unsqueeze(1)), (wkvl[:, 0:2 * C], gates_w[:, C:3 * C]),
                             (wkvl[:, 2 * C:KVW], lr_w), (bkv[:, :], gates_b[C:3 * C].partition_broadcast(P)),
                             (lrb[:, :], lr_b.partition_broadcast(P))):
                sp.dma_start(dst, src).then_inc(kvw_loaded, 16)
            for t in range(1, T):
                sp.dma_start(x_all[:, t], x_v[:, t]).then_inc(x_loaded[1] if t == 1 else x_rest, 16)
            for dst, src in ((b2s[:, :], b2.partition_broadcast(P)), (wq[:, :], gates_w[:, 0:C]), (wo[:, :], out_w),
                             (w1s[:, :], w1), (w2s[:, :], w2), (bo[:, :], out_b.partition_broadcast(P)),
                             (mng, mn_g.unsqueeze(1)), (mnb, mn_b.unsqueeze(1)), (b1c, b1.unsqueeze(1)),
                             (bqc, gates_b[0:C].unsqueeze(1))):
                sp.dma_start(dst, src).then_inc(w_loaded, 16)
            sp.dma_start(gw[:, :], gate_w).then_inc(e_loaded, 16)
            sp.dma_start(ew[:, :, :], expert_w.rearrange("e f h -> f e h")).then_inc(e_loaded, 16)

            def keep_xn(i, s):
                sp.wait_ge(x_loaded[0], 16)
                sp.wait_ge(xnT_ready, 2 * i + s + 1)
                sp.dma_start(xnT_all[:, 2 * i + s, :], xnT[s][:, :]).then_inc(xnT_kept[s], 16)

            def keep_kv(i, s):
                sp.wait_ge(x_loaded[0], 16)
                sp.wait_ge(k_ready, 2 * i + s + 1)
                sp.dma_start(kv_all[:, 2 * i + s, :], kv[s][:, :, :].rearrange("p n c -> p (n c)")).then_inc(kv_kept[s], 16)

            def keep_g(i, s):
                sp.wait_ge(x_loaded[0], 16)
                sp.wait_ge(g_ready, 2 * i + s + 1)
                sp.dma_start(g_all[:, 2 * i + s, :], gg[s][:, :, :].rearrange("p n c -> p (n c)")).then_inc(g_kept[s], 16)

            def first1():
                keep_xn(0, 0)
                keep_xn(0, 1)

            def body1(i, s, ahead2, ahead1):
                nxt = after(i, s)
                keep_kv(i, s)
                if ahead2:
                    keep_xn(i + 1, s)
                keep_g(i, s)

            two_ahead(sp, first1, body1)

            for s in range(2):
                sp.wait_ge(kv_kept[s], 16 * NIT)
                sp.wait_ge(g_kept[s], 16 * NIT)
                sp.wait_ge(xnT_kept[s], 16 * NIT)

            def stage_g(i, s):
                sp.wait_ge(x_loaded[0], 16)
                earlier(sp, y64_mm[s], i)
                sp.dma_start(gs[s][:, :, :].rearrange("p n c -> p (n c)"), g_all[:, 2 * i + s, :]).then_inc(gs_loaded[s], 16)

            def stage_kv(i, s):
                sp.wait_ge(x_loaded[0], 16)
                earlier(sp, sm_mm[NS - 1][s], i)
                sp.dma_start(kvs[s][:, :, :].rearrange("p n c -> p (n c)"), kv_all[:, 2 * i + s, :]).then_inc(kvs_loaded[s], 16)

            def first2():
                stage_g(0, 0)
                stage_kv(0, 0)
                stage_g(0, 1)

            def body2(i, s, ahead2, ahead1):
                nxt = after(i, s)
                if ahead2:
                    stage_g(i + 1, s)
                if ahead1:
                    stage_kv(*nxt)

            two_ahead(sp, first2, body2)

            def stage3(i, s):
                sp.wait_ge(x_loaded[0], 16)
                earlier(sp, dl_mm[s], i)
                sp.dma_start(xns[s][:, :, :].rearrange("p n c -> p (n c)"), xnT_all[:, 2 * i + s, :]).then_inc(xns_loaded[s], 16)

            def store(i, s):
                sp.wait_ge(x_loaded[0], 16)
                for b in range(2):
                    sp.wait_ge(add_step[b], ADDS * (4 * i + 2 * s + 2))
                sp.dma_start(out_v[:, 2 * i + s], x_all[:, 2 * i + s]).then_inc(stored, 16)

            stage3(0, 0)
            stage3(0, 1)
            stage3(1, 0)
            stage3(1, 1)
            store(0, 0)
            with sp.Fori(1, NIT - 1) as i:
                stage3(i + 1, 0)
                store(i - 1, 1)
                stage3(i + 1, 1)
                store(i, 0)
            store(NIT - 2, 1)
            store(NIT - 1, 0)
            store(NIT - 1, 1)
            sp.wait_ge(stored, 16 * T)

        @block.gpsimd
        def _(pool):
            nc.gpsimd.memset(ident[:], 0.0).then_inc(id_zero, 1)
            nc.gpsimd.memset(xi[:], 0.0).then_inc(id_zero, 1)
            pool.wait_ge(id_zero, 2)
            nc.gpsimd.affine_select(out=ident[:], in_=ident[:], compare_op=ALU.not_equal, fill=1.0, base=0,
                                    pattern=[[-1, P]], channel_multiplier=1).then_inc(id_ready, 1)
            nc.gpsimd.affine_select(out=xi[:], in_=xi[:], compare_op=ALU.not_equal, fill=1.0, base=0,
                                    pattern=[[1, Q], [-1, Q]], channel_multiplier=0).then_inc(xi_ready, 1)
            for e in range(E):
                nc.gpsimd.memset(desc[:, e:e + 1], float(E - e)).then_inc(consts_ready, 1)
            nc.gpsimd.memset(epsc[:], EPS).then_inc(consts_ready, 1)
            for s in range(2):
                nc.gpsimd.memset(tt[s][:], 0.0).then_inc(consts_ready, 1)
                nc.gpsimd.memset(da[s][:], 0.0).then_inc(consts_ready, 1)

            pool.wait_ge(xi_ready, 1)
            pool.wait_ge(consts_ready, E + 5)

            pool.wait_ge(w_loaded, 16 * 10)
            b2B = b2s[:, :].unsqueeze(1).broadcast_to([P, NS, C])

            def diagonals(i, s):
                pool.wait_ge(g_ready, 2 * i + s + 1)
                for b in range(NB):
                    r = slice(Q * b, Q * b + Q)
                    nc.gpsimd.tensor_copy(
                        gd_all[r, :, bass.ds((2 * i + s) * NS, NS)].rearrange("p c n -> p n c"),
                        gg[s][r, :, Q * b:Q * b + Q]).then_inc(gd_done[s], 1)
                    pool.wait_ge(gd_done[s], NB * i + b + 1)

            def plus_b2(i, s):
                pool.wait_ge(h_done[s], i + 1)
                nc.gpsimd.tensor_tensor(x_all[:, 2 * i + s], x_all[:, 2 * i + s], b2B, ALU.add)

            def both(i, s):
                diagonals(i, s)
                plus_b2(i, s)

            both(0, 0)
            both(0, 1)
            with pool.Fori(1, NIT - 1) as i:
                both(i, 0)
                both(i, 1)
            both(NIT - 1, 0)
            plus_b2(NIT - 1, 1)

            pool.wait_ge(ewT_ready, 1)
            nc.gpsimd.tensor_tensor(ewT[:], ewT[:], ident[:, :].unsqueeze(1).broadcast_to([P, E, F]), ALU.add).then_inc(ewI_ready, 1)

            pool.wait_ge(cb_ready, 1)

            def sums(i, s, n):
                if not (isinstance(i, int) and 2 * i + s == T - 1 and n == NS - 1):
                    total(pool, nc.gpsimd.tensor_tensor, i, s, n)

            def hcb_(i, s):
                nc.gpsimd.tensor_tensor(h_all[:, 2 * i + s], h_all[:, 2 * i + s], cb[:], ALU.add).then_inc(hcb_ready, 1)

            def xb_(i, s):
                pool.wait_ge(h2_ready[s], i + 1)
                nc.gpsimd.tensor_tensor(x_all[:, 2 * i + s], x_all[:, 2 * i + s], h_all[:, 2 * i + s], ALU.add).then_inc(xb_ready[s], 1)

            def first3():
                hcb_(0, 0)
                xb_(0, 0)
                hcb_(0, 1)
                xb_(0, 1)

            def body3(i, s, ahead2, ahead1):
                nxt = after(i, s)
                if ahead2:
                    hcb_(i + 1, s)
                    xb_(i + 1, s)
                sums(i, s, 0)
                sums(i, s, 1)
                sums(i, s, 2)
                sums(i, s, 3)

            two_ahead(pool, first3, body3)

        @block.scalar
        def _(act):
            def roots1(i, s):
                act.wait_ge(ab_done, 2 * i + s + 1)
                nc.scalar.activation(sd[s][:], ab[s][:], ACT.Sqrt).then_inc(sd_done, 1)

            def h1(i, s):
                act.wait_ge(nb_done, 2 * i + s + 1)
                for n in range(NS):
                    last = nc.scalar.activation(h_all[:, 2 * i + s, n], x_all[:, 2 * i + s, n], ACT.Identity,
                                                bias=nb[s][:, n:n + 1], scale=rr[s][:, 0, n:n + 1])
                last.then_inc(h_done[s], 1)

            def xn1(i, s):
                act.wait_ge(xT_mm[s], i + 1)
                earlier(act, kv_mm[s], NS * i)
                earlier(act, xnT_kept[s], 16 * i)
                nc.scalar.activation(xnT[s][:], ps[:, 0, :], ACT.Identity, bias=dnb, scale=dng).then_inc(xnT_ready, 1)

            def norms1(i, s):
                earlier(act, rn_done[s], i)
                for n in range(NS):
                    act.wait_ge(kv_ready[s], NS * i + n + 1)
                    last = nc.scalar.activation(sq[:, n], kv[s][:, n, 0:C], ACT.Square, accum_out=ss[s][:, n:n + 1])
                last.then_inc(ss_done, 1)
                act.wait_ge(ss_done, 2 * i + s + 1)
                nc.scalar.activation(sn[s][:], ss[s][:], ACT.Sqrt).then_inc(sn_done, 1)

            def kT1(i, s):
                act.wait_ge(kT_mm[s], i + 1)
                earlier(act, g_mm[s], i)
                nc.scalar.copy(kT[s][:], ps[:, 5, :]).then_inc(kT_ready, 1)

            def gram1(i, s):
                act.wait_ge(g_mm[s], i + 1)
                if isinstance(i, int) and 2 * i + s == T - 1:
                    last_diagonals(nc.scalar.copy, 0)
                    act.wait_ge(last_gd_done, NB)
                earlier(act, g_kept[s], 16 * i)
                earlier(act, gd_done[s], NB * i)
                nc.scalar.copy(gg[s][:].rearrange("p n c -> p (n c)"), ps[:, 6, :]).then_inc(g_ready, 1)

            def first1():
                roots1(0, 0)
                act.wait_ge(kvw_loaded, 16 * 6)
                xn1(0, 0)
                roots1(0, 1)
                h1(0, 0)
                xn1(0, 1)
                norms1(0, 0)

            def body1(i, s, ahead2, ahead1):
                nxt = after(i, s)
                if ahead2:
                    roots1(i + 1, s)
                if ahead1:
                    h1(*nxt)
                kT1(i, s)
                if ahead2:
                    xn1(i + 1, s)
                if ahead1:
                    norms1(*nxt)
                gram1(i, s)

            two_ahead(act, first1, body1)

            act.wait_ge(w_loaded, 16 * 10)

            act.wait_ge(wqT_mm, 1)
            nc.scalar.copy(wqT[:], ps[:, 0, 0:C])
            nc.scalar.copy(gwT[:], ps[:, 0, C:C + E]).then_inc(wqT_ready, 1)
            act.wait_ge(ewT_mm, 2)
            for q in range(2):
                last = nc.scalar.copy(ewT[:, EH * q:EH * q + EH, :].rearrange("p e f -> p (e f)"), ps[:, 1 + q, :])
            last.then_inc(ewT_ready, 1)

            def ya(i, s):
                act.wait_ge(ya_mm, 2 * i + s + 1)
                earlier(act, za_mm[s], i)
                nc.scalar.copy(yT[s][0:Q], ps[0:Q, 0, 0:NS * Q]).then_inc(ya_ready, 1)

            def za(i, s):
                act.wait_ge(za_mm[s], i + 1)
                nc.scalar.mul(tt[s][0:Q, :, Q:2 * Q], ps[0:Q, 0, NS * Q:2 * NS * Q].rearrange("p (n c) -> p n c", n=NS), -1.0)
                nc.scalar.mul(da[s][Q:2 * Q, :, 0:Q], ps[Q:2 * Q, 0, 2 * NS * Q:3 * NS * Q].rearrange("p (n c) -> p n c", n=NS),
                              -1.0).then_inc(za_ready, 1)

            def y64_(i, s):
                act.wait_ge(y64_mm[s], i + 1)
                earlier(act, t12_mm[s], i)
                nc.scalar.copy(y64[s][:], ps[0:2 * Q, 2, 0:2 * NS * Q]).then_inc(y64_ready, 1)

            def wT_(i, s):
                act.wait_ge(wT_mm[s], i + 1)
                earlier(act, u_mm[NS - 1], 2 * i)
                nc.scalar.mul(wT[s][:], ps[:, 5, :], -1.0).then_inc(wT_ready, 1)

            def u_(i, s, n):
                act.wait_ge(u_mm[n], 2 * i + s + 1)
                earlier(act, sm_mm[n][1 - s], i + s)
                nc.scalar.copy(uu[:, n, 0:C], tiles(3 + n % 2)[:, n]).then_inc(u_ready[n], 1)

            def tt_(i, s):
                earlier(act, wT_mm[s], i)
                for b in range(NB):
                    r = slice(Q * b, Q * b + Q)
                    last = nc.scalar.copy(tt[s][r, :, Q * b:Q * b + Q],
                                          dT_all[r, :, bass.ds((2 * i + s) * NS, NS)].rearrange("p r n -> p n r"))
                last.then_inc(tt_set, 1)

            act.wait_ge(dT_done, 1)
            act.wait_ge(consts_ready, E + 5)
            def first2():
                tt_(0, 0)
                ya(0, 0)
                za(0, 0)
                y64_(0, 0)

            def body2(i, s, ahead2, ahead1):
                nxt = after(i, s)
                if ahead1:
                    tt_(*nxt)
                    ya(*nxt)
                wT_(i, s)
                if ahead1:
                    za(*nxt)
                u_(i, s, 0)
                u_(i, s, 1)
                if ahead1:
                    y64_(*nxt)
                u_(i, s, 2)
                u_(i, s, 3)

            two_ahead(act, first2, body2)

            act.wait_ge(fold_mm, 1)
            nc.scalar.copy(mT[:], ps[:, 0, :]).then_inc(fold_out, 1)
            act.wait_ge(fold_mm, 2)
            nc.scalar.copy(mw[:], ps[:, 1, :]).then_inc(fold_out, 1)
            act.wait_ge(fold_mm, 4)
            nc.scalar.copy(gn[:].rearrange("p n c -> p (n c)"), ps[:, 2, :]).then_inc(fold_out, 1)

            def root(i, s, second):
                act.wait_ge(mv_done, norms(i, s, second) + 1)
                nc.scalar.activation(sd[s][:, 0], mv[s][:, :, 1], ACT.Sqrt, bias=epsc[:, 0:1]).then_inc(sd_done, 1)

            def tn_(i, s):
                act.wait_ge(nb0_done, 2 * i + s + 1)
                earlier(act, tT_mm[s], i)
                for n in range(2, NS):
                    last = nc.scalar.activation(tnv[s][:, n], h_all[:, 2 * i + s, n], ACT.Identity,
                                                bias=nb0[s][:, n - 2:n - 1], scale=rr[s][:, 0, n:n + 1])
                last.then_inc(tnb_ready, 1)

            def tT_(i, s):
                act.wait_ge(tT_mm[s], i + 1)
                earlier(act, hid_mm[s], i)
                nc.scalar.activation(tT[s][:].rearrange("p n c -> p (n c)"), ps[:, 1, :], ACT.Identity, bias=mnb,
                                     scale=mng).then_inc(tT_ready, 1)

            def hid_(i, s):
                act.wait_ge(hid_mm[s], i + 1)
                earlier(act, out_mm[s], i)
                nc.scalar.activation(hid[s][:].rearrange("p n c -> p (n c)"), ps[:, 2, :], ACT.Relu,
                                     bias=b1c).then_inc(hid_ready, 1)

            def zT_(i, s):
                act.wait_ge(zT_mm[s], i + 1)
                nc.scalar.copy(zT[s][:].rearrange("p n c -> p (n c)"), ps[:, 1, :]).then_inc(zT_ready, 1)

            def zs_(i, s):
                earlier(act, zT_mm[s], i)
                act.wait_ge(nb_done, T + 2 * i + s + 1)
                for n in range(NS):
                    last = nc.scalar.activation(zv[s][:, n], x_all[:, 2 * i + s, n], ACT.Identity, bias=nb[s][:, n:n + 1],
                                                scale=rr[s][:, 0, n:n + 1])
                last.then_inc(z_ready, 1)

            def mask(i, s, n):
                b, k = n % 2, 4 * i + 2 * s + n // 2
                act.wait_ge(oh_ready, 2 * i + s + 1)
                act.wait_ge(ea_mm[b], k + 1)
                earlier(act, sum_done[b], k)
                for e in range(EH):
                    last = nc.scalar.activation(ea[b][:, e], ps[:, 4 + 2 * b, e * F:e * F + F], ACT.Copy,
                                                scale=oh[s][:, n, e:e + 1])
                last.then_inc(ea_done[b], 1)

            def first3():
                root(0, 0, 0)
                tn_(0, 0)
                tT_(0, 0)
                hid_(0, 0)
                root(0, 0, 1)
                zs_(0, 0)
                root(0, 1, 0)
                zT_(0, 0)
                tn_(0, 1)
                tT_(0, 1)

            def body3(i, s, ahead2, ahead1):
                nxt = after(i, s)
                if ahead1:
                    hid_(*nxt)
                mask(i, s, 0)
                if ahead1:
                    root(*nxt, 1)
                mask(i, s, 1)
                if ahead1:
                    zs_(*nxt)
                if ahead2:
                    root(i + 1, s, 0)
                if ahead1:
                    zT_(*nxt)
                if ahead2:
                    tn_(i + 1, s)
                mask(i, s, 2)
                if ahead2:
                    tT_(i + 1, s)
                mask(i, s, 3)

            two_ahead(act, first3, body3)

        @block.vector
        def _(dve):
            bkvB = bkv[:, :]
            nc.vector.memset(sm[:], 0.0).then_inc(sm_ready[0], 1)

            def stats(s, k, src):
                dve.sem_inc(dve_passed, 1)
                for n in range(NS):
                    last = nc.vector.bn_stats(st[s][:, n], src(n))
                last.then_inc(stats_done, 1)

            def moments(s, k):
                dve.wait_ge(stats_done, k + 1)
                dve.sem_inc(dve_passed, 1)
                for n in range(NS):
                    last = nc.vector.bn_aggr(mv[s][:, n], st[s][:, n])
                last.then_inc(mv_done, 1)

            def stats1(i, s):
                stats(s, 2 * i + s, lambda n: x_all[:, 2 * i + s, n])

            def moments1(i, s):
                moments(s, 2 * i + s)
                dve.wait_ge(mv_done, 2 * i + s + 1)
                nc.vector.tensor_scalar(ab[s][:, 0], mv[s][:, :, 1], EPS, None, ALU.add)
                nc.vector.tensor_scalar(ab[s][:, 1], mv[s][:, :, 1], 1.0 + EPS, EPS * EPS, ALU.mult, ALU.add).then_inc(ab_done, 1)

            def scale1(i, s):
                dve.wait_ge(sd_done, 2 * i + s + 1)
                earlier(dve, h_done[s], i)
                nc.vector.reciprocal(rr[s][:], sd[s][:]).then_inc(rr_done, 1)
                dve.wait_ge(rr_done, 2 * i + s + 1)
                nc.vector.scalar_tensor_tensor(nb[s][:], mv[s][:, :, 0], -1.0, rr[s][:, 0], ALU.mult,
                                               ALU.mult).then_inc(nb_done, 1)
                earlier(dve, xT_mm[s], i)
                for n in range(NS):
                    last = nc.vector.tensor_scalar(xh[s][:, n], x_all[:, 2 * i + s, n], mv[s][:, n, 0:1],
                                                   rr[s][:, 1, n:n + 1], ALU.subtract, ALU.mult)
                last.then_inc(xh_ready, 1)

            def kv1(i, s):
                earlier(dve, kv_kept[s], 16 * i)
                earlier(dve, kT_mm[s], i)
                for n in range(NS):
                    dve.wait_ge(kv_mm[s], NS * i + n + 1)
                    nc.vector.tensor_tensor(kv[s][:, n], ps[:, 1 + n, 0:2 * C], bkvB, ALU.add).then_inc(kv_ready[s], 1)
                nc.vector.tensor_scalar(lr_all[:, bass.ds((2 * i + s) * NS, NS)], ps[:, 1:1 + NS, 2 * C], lrb[:, 0:1], None,
                                        ALU.add).then_inc(lr_ready, 1)

            def norm1(i, s):
                dve.wait_ge(sn_done, 2 * i + s + 1)
                nc.vector.reciprocal(rn[s][:], sn[s][:]).then_inc(rn_done[s], 1)

            def k1(i, s):
                dve.wait_ge(rn_done[s], i + 1)
                dve.wait_ge(kv_ready[s], NS * (i + 1))
                for n in range(NS):
                    last = nc.vector.tensor_scalar(kv[s][:, n, 0:C], kv[s][:, n, 0:C], rn[s][:, n:n + 1], None, ALU.mult)
                last.then_inc(k_ready, 1)

            def first1():
                dve.wait_ge(x_loaded[0], 16)
                stats1(0, 0)
                moments1(0, 0)
                scale1(0, 0)
                dve.wait_ge(x_loaded[1], 16)
                stats1(0, 1)
                moments1(0, 1)
                scale1(0, 1)
                dve.wait_ge(x_rest, 16 * (T - 2))
                dve.wait_ge(kvw_loaded, 16 * 6)

            def body1(i, s, ahead2, ahead1):
                nxt = after(i, s)
                kv1(i, s)
                if ahead2:
                    stats1(i + 1, s)
                    moments1(i + 1, s)
                norm1(i, s)
                k1(i, s)
                if ahead2:
                    scale1(i + 1, s)

            two_ahead(dve, first1, body1)

            dve.wait_ge(w_loaded, 16 * 10)
            nc.vector.tensor_copy(bqB[:], bqc.broadcast_to([P, P])).then_inc(bqB_ready, 1)

            dve.wait_ge(g_mm[1], NIT)
            last_diagonals(nc.vector.tensor_copy, 2)

            dve.wait_ge(gd_done[0], NB * NIT)
            dve.wait_ge(gd_done[1], NB * (NIT - 1))
            dve.wait_ge(last_gd_done, NB)
            nc.vector.transpose(lt[:].rearrange("p c r -> p (c r)"), gd_all[:].rearrange("p c t -> p (c t)")).then_inc(lt_done, 1)
            dve.wait_ge(lt_done, 1)
            dve.wait_ge(xi_ready, 1)
            done, sub_at = 0, [0, 0]
            for j in range(Q - 1):
                m, w = Q - 1 - j, j + 1
                top = m if m * w < 2 * Q else (m + 1) // 2
                halves = [(half, lo, hi) for half, lo, hi in ((0, j + 1, j + 1 + top), (1, j + 1 + top, Q)) if hi > lo]
                mul_at, mul = [0, 0], {}
                for half, lo, hi in halves:
                    mul[half] = prod[:, half * (Q * Q // 2):half * (Q * Q // 2) + (hi - lo) * w].rearrange("p (i k) -> p i k", k=w)
                    earlier(dve, elim, sub_at[half])
                    nc.vector.tensor_tensor(mul[half], lt[:, j, lo:hi].unsqueeze(2).broadcast_to([P, hi - lo, w]),
                                            xi[:, j, 0:w].unsqueeze(1).broadcast_to([P, hi - lo, w]),
                                            ALU.mult).then_inc(elim, 1)
                    done += 1
                    mul_at[half] = done
                for half, lo, hi in halves:
                    dve.wait_ge(elim, mul_at[half])
                    nc.vector.tensor_tensor(xi[:, lo:hi, 0:w], xi[:, lo:hi, 0:w], mul[half], ALU.subtract).then_inc(elim, 1)
                    done += 1
                    sub_at[half] = done
                sub_at[1] = max(sub_at)
            dve.wait_ge(elim, done)
            nc.vector.transpose(dT_all[:].rearrange("p r t -> p (r t)"), xi[:].rearrange("p r c -> p (r c)")).then_inc(dT_done, 1)
            nc.vector.transpose(d_all[:], xi[:].rearrange("p r c -> p c r")).then_inc(d_done, 1)

            def yb(i, s):
                dve.wait_ge(yb_mm, 2 * i + s + 1)
                earlier(dve, zb_mm[s], i)
                nc.vector.tensor_copy(yT[s][2 * Q:3 * Q].rearrange("p n c -> p (n c)"),
                                      ps[2 * Q:3 * Q, 1, 0:NS * Q]).then_inc(yb_ready, 1)

            def zb(i, s):
                dve.wait_ge(zb_mm[s], i + 1)
                nc.vector.tensor_scalar(tt[s][2 * Q:3 * Q, :, 3 * Q:4 * Q],
                                        ps[2 * Q:3 * Q, 1, NS * Q:2 * NS * Q].rearrange("p (n c) -> p n c", n=NS), -1.0, None,
                                        ALU.mult).then_inc(zb_ready, 1)

            def t12(i, s):
                dve.wait_ge(t12_mm[s], i + 1)
                nc.vector.tensor_scalar(tt[s][0:2 * Q, :, 2 * Q:4 * Q],
                                        ps[0:2 * Q, 2, 2 * NS * Q:4 * NS * Q].rearrange("p (n c) -> p n c", n=NS), -1.0, None,
                                        ALU.mult).then_inc(t12_ready, 1)

            def lru(i, s, n):
                dve.wait_ge(u_ready[n], 2 * i + s + 1)
                nc.vector.tensor_scalar(uu[:, n, C:2 * C], uu[:, n, 0:C], lr_all[:, bass.ds((2 * i + s) * NS + n, 1)], None,
                                        ALU.mult).then_inc(lru_ready[n], 1)

            def add_sm(i, s, n):
                dve.wait_ge(sm_mm[n][s], i + 1)
                nc.vector.tensor_tensor(sm[:, n], ps[:, 6 + n % 2, 0:2 * C], sm[:, n], ALU.add).then_inc(sm_ready[n], 1)

            def da_(i, s):
                earlier(dve, t12_mm[s], i)
                at = bass.ds((2 * i + s) * NS, NS)
                for b in range(NB - 1):
                    r = slice(Q * b, Q * b + Q)
                    last = nc.vector.tensor_copy(da[s][r, :, Q * (b % 2):Q * (b % 2) + Q], d_all[r, :, at].rearrange("p r n -> p n r"))
                last.then_inc(da_set, 1)

            dve.wait_ge(d_done, 1)
            dve.wait_ge(consts_ready, E + 5)
            def first2():
                da_(0, 0)
                yb(0, 0)
                zb(0, 0)
                t12(0, 0)
                da_(0, 1)
                yb(0, 1)
                zb(0, 1)
                lru(0, 0, 0)
                lru(0, 0, 1)

            def body2(i, s, ahead2, ahead1):
                nxt = after(i, s)
                lru(i, s, 2)
                add_sm(i, s, 0)
                if ahead1:
                    t12(*nxt)
                if ahead2:
                    da_(i + 1, s)
                lru(i, s, 3)
                add_sm(i, s, 1)
                add_sm(i, s, 2)
                if ahead2:
                    yb(i + 1, s)
                add_sm(i, s, 3)
                if ahead2:
                    zb(i + 1, s)
                if ahead1:
                    lru(*nxt, 0)
                    lru(*nxt, 1)

            two_ahead(dve, first2, body2)

            dve.wait_ge(fold_mm, 3)
            nc.vector.tensor_tensor(cb[:], tiles(3), bo[:, :].unsqueeze(1).broadcast_to([P, NS, C]), ALU.add).then_inc(cb_ready, 1)

            def inverse_root(i, s, second):
                k = norms(i, s, second)
                dve.wait_ge(sd_done, k + 1)
                nc.vector.reciprocal(rr[s][:, 0], sd[s][:, 0]).then_inc(rr_done, 1)

            def resid(i, s):
                dve.wait_ge(dl_mm[s], i + 1)
                dve.wait_ge(hcb_ready, 2 * i + s + 1)
                nc.vector.tensor_tensor(h_all[:, 2 * i + s], tiles(0), h_all[:, 2 * i + s], ALU.add).then_inc(h2_ready[s], 1)

            def resid_stats(i, s):
                dve.wait_ge(h2_ready[s], i + 1)
                stats(s, norms(i, s, 0), lambda n: h_all[:, 2 * i + s, n])

            def shift(i, s):
                dve.wait_ge(rr_done, norms(i, s, 0) + 1)
                nc.vector.scalar_tensor_tensor(nb0[s][:], mv[s][:, 2:4, 0], -1.0, rr[s][:, 0, 2:4], ALU.mult,
                                               ALU.mult).then_inc(nb0_done, 1)

            def tn_(i, s):
                dve.wait_ge(rr_done, norms(i, s, 0) + 1)
                earlier(dve, tT_mm[s], i)
                for n in range(2):
                    last = nc.vector.tensor_scalar(tnv[s][:, n], h_all[:, 2 * i + s, n], mv[s][:, n, 0:1], rr[s][:, 0, n:n + 1],
                                                   ALU.subtract, ALU.mult)
                last.then_inc(tn_ready, 1)

            def mlp_out(i, s):
                dve.wait_ge(out_mm[s], i + 1)
                dve.wait_ge(xb_ready[s], i + 1)
                nc.vector.tensor_tensor(x_all[:, 2 * i + s], tiles(2), x_all[:, 2 * i + s], ALU.add).then_inc(x1_ready[s], 1)

            def x1_stats(i, s):
                dve.wait_ge(x1_ready[s], i + 1)
                stats(s, norms(i, s, 1), lambda n: x_all[:, 2 * i + s, n])

            def zscale(i, s):
                dve.wait_ge(rr_done, norms(i, s, 1) + 1)
                nc.vector.scalar_tensor_tensor(nb[s][:], mv[s][:, :, 0], -1.0, rr[s][:, 0], ALU.mult,
                                               ALU.mult).then_inc(nb_done, 1)

            def choose(i, s, step):
                scores = ps[:, 3, 0:NS * E].rearrange("p (n e) -> p n e", n=NS)
                if step == 1:
                    dve.wait_ge(gate_mm, 2 * i + s + 1)
                    nc.vector.tensor_reduce(mx[s][:], scores, AX_X, ALU.max).then_inc(oh_step[s], 1)
                    return
                dve.wait_ge(oh_step[s], 4 * i + step - 1)
                if step == 2:
                    nc.vector.tensor_tensor(eq[s][:], scores, mx[s][:].unsqueeze(2).broadcast_to([P, NS, E]),
                                            ALU.is_equal).then_inc(oh_step[s], 1)
                elif step == 3:
                    nc.vector.tensor_tensor(eq[s][:], eq[s][:], desc[:, :].unsqueeze(1).broadcast_to([P, NS, E]),
                                            ALU.mult).then_inc(oh_step[s], 1)
                elif step == 4:
                    nc.vector.tensor_reduce(m2[s][:], eq[s][:], AX_X, ALU.max).then_inc(oh_step[s], 1)
                else:
                    nc.vector.tensor_tensor(oh[s][:], eq[s][:], m2[s][:].unsqueeze(2).broadcast_to([P, NS, E]),
                                            ALU.is_equal).then_inc(oh_ready, 1)

            def mask(i, s, n):
                b, k = n % 2, 4 * i + 2 * s + n // 2
                dve.wait_ge(oh_ready, 2 * i + s + 1)
                dve.wait_ge(ed_mm[b], k + 1)
                earlier(dve, sum_done[b], k)
                nc.vector.tensor_tensor(ed[b], ps[:, 5 + 2 * b, :].rearrange("p (e f) -> p e f", e=EH),
                                        oh[s][:, n, EH:E].unsqueeze(2).broadcast_to([P, EH, F]), ALU.mult).then_inc(ed_done[b], 1)

            def join(i, s, n):
                b, k = n % 2, 4 * i + 2 * s + n // 2
                dve.wait_ge(ed_done[b], k + 1)
                dve.wait_ge(ea_done[b], k + 1)
                earlier(dve, add_step[b], ADDS * k)
                nc.vector.tensor_tensor(es[b], ed[b], ea[b], ALU.add).then_inc(sum_done[b], 1)

            def first3():
                resid(0, 0)
                resid_stats(0, 0)
                moments(0, norms(0, 0, 0))
                inverse_root(0, 0, 0)
                shift(0, 0)
                tn_(0, 0)
                mlp_out(0, 0)
                x1_stats(0, 0)
                moments(0, norms(0, 0, 1))
                resid(0, 1)
                inverse_root(0, 0, 1)
                zscale(0, 0)
                resid_stats(0, 1)
                moments(1, norms(0, 1, 0))
                inverse_root(0, 1, 0)
                shift(0, 1)
                tn_(0, 1)

            def body3(i, s, ahead2, ahead1):
                nxt = after(i, s)
                choose(i, s, 1)
                choose(i, s, 2)
                choose(i, s, 3)
                choose(i, s, 4)
                choose(i, s, 5)
                if ahead1:
                    mlp_out(*nxt)
                    x1_stats(*nxt)
                    moments(nxt[1], norms(*nxt, 1))
                if ahead2:
                    resid(i + 1, s)
                if ahead1:
                    inverse_root(*nxt, 1)
                    zscale(*nxt)
                mask(i, s, 0)
                if ahead2:
                    resid_stats(i + 1, s)
                join(i, s, 0)
                if ahead2:
                    moments(s, norms(i + 1, s, 0))
                mask(i, s, 1)
                if ahead2:
                    inverse_root(i + 1, s, 0)
                    shift(i + 1, s)
                join(i, s, 1)
                if ahead2:
                    tn_(i + 1, s)
                mask(i, s, 2)
                join(i, s, 2)
                mask(i, s, 3)
                join(i, s, 3)

            dve.wait_ge(consts_ready, E + 5)
            two_ahead(dve, first3, body3)
            total(dve, nc.vector.tensor_tensor, NIT - 1, 1, NS - 1)

        @block.tensor
        def _(pe):
            pe.wait_ge(id_ready, 1)
            pe.wait_ge(kvw_loaded, 16 * 6)

            def four(bank, lhsT, rhs, ready, step=1):
                for n in range(NS):
                    last = nc.tensor.matmul(tiles(bank)[:, n], lhsT(n), rhs(n), start=True, stop=True)
                last.then_inc(ready, step)

            def turn(bank, src, ready):
                for n in range(NS):
                    last = nc.tensor.transpose(tiles(bank)[:, n], src(n), ident[:])
                last.then_inc(ready, 1)

            def xT1(i, s):
                pe.wait_ge(xh_ready, 2 * i + s + 1)
                earlier(pe, xnT_ready, 2 * i + s)
                turn(0, lambda n: xh[s][:, n], xT_mm[s])

            def kvm1(i, s):
                pe.wait_ge(xnT_ready, 2 * i + s + 1)
                earlier(pe, lr_ready, 2 * i + s)
                for n in range(NS):
                    nc.tensor.matmul(ps[:, 1 + n, 0:KVW], xnT[s][:, n * P:n * P + P], wkvl[:], start=True,
                                     stop=True).then_inc(kv_mm[s], 1)

            def kT1(i, s):
                pe.wait_ge(k_ready, 2 * i + s + 1)
                earlier(pe, kT_ready, 2 * i + s)
                turn(5, lambda n: kv[s][:, n, 0:C], kT_mm[s])

            def gram1(i, s):
                pe.wait_ge(kT_ready, 2 * i + s + 1)
                earlier(pe, g_ready, 2 * i + s)
                four(6, lambda n: kT[s][:, n * P:n * P + P], lambda n: kT[s][:, n * P:n * P + P], g_mm[s])

            def first1():
                xT1(0, 0)
                kvm1(0, 0)
                xT1(0, 1)

            def body1(i, s, ahead2, ahead1):
                nxt = after(i, s)
                if ahead1:
                    kvm1(*nxt)
                kT1(i, s)
                if ahead2:
                    xT1(i + 1, s)
                gram1(i, s)

            two_ahead(pe, first1, body1)

            pe.wait_ge(xnT_ready, T)
            pe.wait_ge(lr_ready, T)
            pe.wait_ge(e_loaded, 32)
            pe.wait_ge(w_loaded, 16 * 10)
            nc.tensor.transpose(ps[:, 0, 0:C], wq[:], ident[:])
            nc.tensor.transpose(ps[:, 0, C:C + E], gw[:], ident[0:E, 0:E]).then_inc(wqT_mm, 1)
            for q in range(2):
                turn(1 + q, lambda n: ew[:, EH * q + n], ewT_mm)

            pe.wait_ge(wqT_ready, 1)
            pe.wait_ge(ewT_ready, 1)
            pe.wait_ge(kT_ready, T)
            pe.wait_ge(g_ready, T)

            def ya(i, s):
                pe.wait_ge(tt_set, 2 * i + s + 1)
                pe.wait_ge(gs_loaded[s], 16 * (i + 1))
                earlier(pe, za_ready, 2 * i + s)
                earlier(pe, zb_ready, 2 * i + s)
                pe.sem_inc(pe_passed, 1)
                for bank, lo, ready in ((0, 0, ya_mm), (1, 2 * Q, yb_mm)):
                    hi = lo + Q
                    for n in range(NS):
                        last = nc.tensor.matmul(ps[lo:lo + Q, bank, n * Q:n * Q + Q], gs[s][hi:hi + Q, n, lo:lo + Q],
                                                tt[s][hi:hi + Q, n, hi:hi + Q], start=True, stop=True)
                    last.then_inc(ready, 1)

            def za(i, s):
                pe.wait_ge(ya_ready, 2 * i + s + 1)
                pe.wait_ge(da_set, 2 * i + s + 1)
                pe.sem_inc(pe_passed, 1)
                for n in range(NS):
                    nc.tensor.matmul(ps[0:Q, 0, (NS + n) * Q:(NS + n + 1) * Q], da[s][0:Q, n, 0:Q], yT[s][0:Q, n],
                                     start=True, stop=True)
                for n in range(NS):
                    last = nc.tensor.matmul(ps[Q:2 * Q, 0, (2 * NS + n) * Q:(2 * NS + n + 1) * Q], yT[s][0:Q, n],
                                            da[s][0:Q, n, 0:Q], start=True, stop=True)
                last.then_inc(za_mm[s], 1)
                pe.wait_ge(yb_ready, 2 * i + s + 1)
                pe.sem_inc(pe_passed, 1)
                for n in range(NS):
                    last = nc.tensor.matmul(ps[2 * Q:3 * Q, 1, (NS + n) * Q:(NS + n + 1) * Q], da[s][2 * Q:3 * Q, n, 0:Q],
                                            yT[s][2 * Q:3 * Q, n], start=True, stop=True)
                last.then_inc(zb_mm[s], 1)

            def y64_(i, s):
                pe.wait_ge(zb_ready, 2 * i + s + 1)
                earlier(pe, t12_ready, 2 * i + s)
                pe.sem_inc(pe_passed, 1)
                for n in range(NS):
                    last = nc.tensor.matmul(ps[0:2 * Q, 2, 2 * n * Q:2 * (n + 1) * Q], gs[s][2 * Q:4 * Q, n, 0:2 * Q],
                                            tt[s][2 * Q:4 * Q, n, 2 * Q:4 * Q], start=True, stop=True)
                last.then_inc(y64_mm[s], 1)

            def t12(i, s):
                pe.wait_ge(y64_ready, 2 * i + s + 1)
                pe.wait_ge(za_ready, 2 * i + s + 1)
                pe.sem_inc(pe_passed, 1)
                for n in range(NS):
                    last = nc.tensor.matmul(ps[0:2 * Q, 2, 2 * (NS + n) * Q:2 * (NS + n + 1) * Q], da[s][0:2 * Q, n, :],
                                            y64[s][:, n], start=True, stop=True)
                last.then_inc(t12_mm[s], 1)

            def uv(i, s):
                pe.wait_ge(t12_ready, 2 * i + s + 1)
                pe.wait_ge(kvs_loaded[s], 16 * (i + 1))
                earlier(pe, u_ready[2], 2 * i + s)
                earlier(pe, u_ready[3], 2 * i + s)
                for n in range(NS):
                    nc.tensor.matmul(tiles(3 + n % 2)[:, n], tt[s][:, n], kvs[s][:, n, C:2 * C], start=n < 2, stop=False,
                                     skip_group_check=True)

            def wT_(i, s):
                pe.wait_ge(t12_ready, 2 * i + s + 1)
                pe.wait_ge(kvs_loaded[s], 16 * (i + 1))
                earlier(pe, wT_ready, 2 * i + s)
                four(5, lambda n: kvs[s][:, n, 0:C], lambda n: tt[s][:, n], wT_mm[s])

            def u_(i, s, n):
                if n == 0:
                    pe.wait_ge(wT_ready, 2 * i + s + 1)
                if n >= 2:
                    pe.wait_ge(u_ready[n - 2], 2 * i + s + 1)
                earlier(pe, sm_ready[n], 2 * i + s + (1 if n == 0 else 0))
                nc.tensor.matmul(tiles(3 + n % 2)[:, n], wT[s][:, n], sm[:, n, 0:C], start=False, stop=True,
                                 skip_group_check=True).then_inc(u_mm[n], 1)

            def sm_(i, s, n):
                pe.wait_ge(lru_ready[n], 2 * i + s + 1)
                if n >= 2:
                    pe.wait_ge(sm_ready[n - 2], 2 * i + s + (2 if n == 2 else 1))
                nc.tensor.matmul(ps[:, 6 + n % 2, 0:2 * C], kvs[s][:, n, 0:C], uu[:, n], start=True,
                                 stop=True).then_inc(sm_mm[n][s], 1)

            def first2():
                ya(0, 0)
                za(0, 0)
                y64_(0, 0)
                t12(0, 0)
                ya(0, 1)
                uv(0, 0)
                wT_(0, 0)
                za(0, 1)
                pe.wait_ge(sm_ready[0], 1)
                u_(0, 0, 0)

            def body2(i, s, ahead2, ahead1):
                nxt = after(i, s)
                u_(i, s, 1)
                if ahead1:
                    y64_(*nxt)
                u_(i, s, 2)
                u_(i, s, 3)
                sm_(i, s, 0)
                if ahead1:
                    t12(*nxt)
                sm_(i, s, 1)
                sm_(i, s, 2)
                if ahead2:
                    ya(i + 1, s)
                if ahead1:
                    uv(*nxt)
                    wT_(*nxt)
                sm_(i, s, 3)
                if ahead2:
                    za(i + 1, s)
                if ahead1:
                    u_(*nxt, 0)

            two_ahead(pe, first2, body2)

            for n in range(NS):
                pe.wait_ge(sm_ready[n], T + (1 if n == 0 else 0))
            turn(0, lambda n: sm[:, n, C:2 * C], fold_mm)
            pe.wait_ge(fold_out, 1)
            four(1, lambda n: mT[:, n * C:n * C + C], lambda n: wo[:], fold_mm)
            pe.wait_ge(fold_out, 2)
            pe.wait_ge(bqB_ready, 1)
            nc.tensor.matmul(ps[:, 3, :], bqB[:], mw[:], start=True, stop=True).then_inc(fold_mm, 1)
            nc.tensor.matmul(ps[:, 2, :], wqT[:], mw[:], start=True, stop=True).then_inc(fold_mm, 1)
            pe.wait_ge(fold_out, 3)
            pe.wait_ge(cb_ready, 1)

            def delta(i, s):
                pe.wait_ge(xns_loaded[s], 16 * (i + 1))
                earlier(pe, h2_ready[1 - s], i + s)
                four(0, lambda n: xns[s][:, n], lambda n: gn[:, n], dl_mm[s])

            def tT_(i, s):
                pe.wait_ge(tn_ready, 2 * i + s + 1)
                pe.wait_ge(tnb_ready, 2 * i + s + 1)
                earlier(pe, zT_ready, 2 * i + s)
                turn(1, lambda n: tnv[s][:, n], tT_mm[s])

            def hid_(i, s):
                pe.wait_ge(tT_ready, 2 * i + s + 1)
                earlier(pe, x1_ready[1 - s], i + s)
                nc.tensor.matmul(ps[:, 2, :], w1s[:], tT[s][:].rearrange("p n c -> p (n c)"), start=True,
                                 stop=True).then_inc(hid_mm[s], 1)

            def out_(i, s):
                pe.wait_ge(hid_ready, 2 * i + s + 1)
                four(2, lambda n: hid[s][:, n], lambda n: w2s[:], out_mm[s])

            def zT_(i, s):
                pe.wait_ge(z_ready, 2 * i + s + 1)
                pe.wait_ge(tT_ready, 2 * i + s + 1)
                turn(1, lambda n: zv[s][:, n], zT_mm[s])

            def gate(i, s):
                pe.wait_ge(zT_ready, 2 * i + s + 1)
                earlier(pe, oh_ready, 2 * i + s)
                for n in range(NS):
                    last = nc.tensor.matmul(ps[:, 3, n * E:n * E + E], zT[s][:, n], gwT[:], start=True, stop=True)
                last.then_inc(gate_mm, 1)

            def experts(i, s, n):
                b, k = n % 2, 4 * i + 2 * s + n // 2
                for half, bank, used, ready in ((0, 4 + 2 * b, ea_done, ea_mm), (1, 5 + 2 * b, ed_done, ed_mm)):
                    earlier(pe, used[b], k)
                    nc.tensor.matmul(ps[:, bank, :], zT[s][:, n],
                                     ewT[:, EH * half:EH * half + EH, :].rearrange("p e f -> p (e f)"), start=True,
                                     stop=True).then_inc(ready[b], 1)

            def first3():
                delta(0, 0)
                tT_(0, 0)
                delta(0, 1)
                hid_(0, 0)
                out_(0, 0)
                zT_(0, 0)

            def body3(i, s, ahead2, ahead1):
                nxt = after(i, s)
                if ahead1:
                    tT_(*nxt)
                if ahead2:
                    delta(i + 1, s)
                if ahead1:
                    hid_(*nxt)
                gate(i, s)
                if ahead1:
                    out_(*nxt)
                experts(i, s, 0)
                experts(i, s, 1)
                experts(i, s, 2)
                if ahead1:
                    zT_(*nxt)
                experts(i, s, 3)

            pe.wait_ge(ewI_ready, 1)
            two_ahead(pe, first3, body3)


_INS = ["x", "dn_g", "dn_b", "gates_w", "gates_b", "lr_w", "lr_b", "out_w", "out_b", "mn_g", "mn_b", "w1", "b1", "w2", "b2"]


def kernel(**inputs):
    import numpy as _np
    import concourse.bacc as _bacc
    from concourse import mybir as _mybir
    from concourse.bass_utils import run_bass_kernel_spmd as _run

    nc = _bacc.Bacc("TRN2", target_bir_lowering=False, num_devices=1)
    arrays, args = {}, []
    for name in [f"L0_attn_{n}" for n in _INS] + ["L0_ffn_gate_w", "L0_ffn_expert_w"]:
        a = _np.ascontiguousarray(inputs[name])
        arrays[f"in_{name}_dram"] = a
        args.append(nc.dram_tensor(f"in_{name}_dram", a.shape, _mybir.dt.from_np(a.dtype), kind="ExternalInput").ap())
    shape = inputs["L0_attn_x"].shape
    args.append(nc.dram_tensor("out_dram", shape, _mybir.dt.float32, kind="ExternalOutput").ap())
    delta_block_kernel(nc, *args)
    r = _run(nc, [arrays], core_ids=[0])
    return r.results[0]["out_dram"]
```
